# Optimizing a Trainium2 kernel written in Bass

```python
import numpy as np
import jax
import jax.numpy as jnp

def _softmax(x, axis=-1):
    return jax.nn.softmax(x, axis=axis)

def _gelu(x):
    return jax.nn.gelu(x, approximate=True)

def _silu(x):
    return jax.nn.silu(x)

def _sigmoid(x):
    return jax.nn.sigmoid(x)

def _layernorm(x, axis=-1, eps=1e-05):
    m = jnp.mean(x, axis=axis, keepdims=True)
    v = jnp.var(x, axis=axis, keepdims=True)
    return (x - m) / jnp.sqrt(v + eps)

def _scatter_add(tgt, idx, src, axis=0):
    return tgt.at[idx].add(src)

def _segment_sum(src, seg, n):
    return jax.ops.segment_sum(src, seg, n)
kernel_name = 'mk_vit_tower_d1_tok_img768_r4_74b2d3'

def setup_inputs(seed: int=0):
    np.random.seed(seed)
    _w = jnp.asarray

    def _rec_inputs():
        import jax
        import jax.numpy as jnp
        _rk = jax.random.key(seed)
        x = -0.000221324 + 1.00063 * jax.random.normal(jax.random.fold_in(_rk, 1), (128, 3, 128, 128), jnp.float32)
        return x
    x = _rec_inputs()

    def _L0_tok_setup():
        import jax, jax.numpy as jnp
        import numpy as np
        from jax import lax
        B, C, H, W = (8, 3, 128, 128)
        S, D = (196, 192)
        key = jax.random.key(seed)
        ks = jax.random.split(key, 6)
        return {'img': jax.random.normal(ks[0], (B, C, H, W), dtype=jnp.float32), 'conv_w': jax.random.normal(ks[1], (S, C, 3, 3), dtype=jnp.float32) * 0.1, 'conv_b': jax.random.normal(ks[2], (S,), dtype=jnp.float32) * 0.1, 'score_w': jax.random.normal(ks[3], (C,), dtype=jnp.float32), 'embed_w': jax.random.normal(ks[4], (C, D), dtype=jnp.float32) * 0.1, 'embed_b': jax.random.normal(ks[5], (D,), dtype=jnp.float32) * 0.1}
    _L0_tok_all = _L0_tok_setup()
    _L0_tok_in = {k: v for k, v in _L0_tok_all.items() if k in ('conv_w', 'conv_b', 'score_w', 'embed_w', 'embed_b')}
    del _L0_tok_all

    def _L0_attn_setup():
        import jax, jax.numpy as jnp
        import numpy as np
        B, T, DM = (4, 512, 192)
        H, D = (4, 64)
        DIM = H * D

        def _feature_map(x):
            return jax.nn.elu(x) + 1.0
        key = jax.random.key(seed)
        kx, kq, kk, kv, ko, kg = jax.random.split(key, 6)
        s = 0.02
        return {'x': jax.random.normal(kx, (B, T, DM), jnp.float32), 'Wq': jax.random.normal(kq, (DM, DIM), jnp.float32) * s, 'Wk': jax.random.normal(kk, (DM, DIM), jnp.float32) * s, 'Wv': jax.random.normal(kv, (DM, DIM), jnp.float32) * s, 'Wo': jax.random.normal(ko, (DIM, DM), jnp.float32) * s, 'Wg': jax.random.normal(kg, (DM, DM), jnp.float32) * s}
    _L0_attn_all = _L0_attn_setup()
    _L0_attn_in = {k: v for k, v in _L0_attn_all.items() if k in ('Wq', 'Wk', 'Wv', 'Wo', 'Wg')}
    del _L0_attn_all

    def _L0_ffn_setup():
        import jax, jax.numpy as jnp
        import numpy as np
        B, S, H = (4, 2048, 192)
        E, K = (8, 2)
        key = jax.random.key(seed)
        ks = jax.random.split(key, 5)
        scale = 1.0 / np.sqrt(H)
        x = jax.random.normal(ks[0], (B, S, H), dtype=jnp.float32)
        router_w = jax.random.uniform(ks[1], (E, H), jnp.float32, -scale, scale)
        router_b = jax.random.uniform(ks[2], (E,), jnp.float32, -scale, scale)
        expert_w = jax.random.uniform(ks[3], (E, H, H), jnp.float32, -scale, scale)
        expert_b = jax.random.uniform(ks[4], (E, H), jnp.float32, -scale, scale)
        return {'x': x, 'router_w': router_w, 'router_b': router_b, 'expert_w': expert_w, 'expert_b': expert_b}
    _L0_ffn_all = _L0_ffn_setup()
    _L0_ffn_in = {k: v for k, v in _L0_ffn_all.items() if k in ('router_w', 'router_b', 'expert_w', 'expert_b')}
    del _L0_ffn_all
    return {'x': x, 'L0_tok_conv_w': _L0_tok_in['conv_w'], 'L0_tok_conv_b': _L0_tok_in['conv_b'], 'L0_tok_score_w': _L0_tok_in['score_w'], 'L0_tok_embed_w': _L0_tok_in['embed_w'], 'L0_tok_embed_b': _L0_tok_in['embed_b'], 'L0_attn_Wq': _L0_attn_in['Wq'], 'L0_attn_Wk': _L0_attn_in['Wk'], 'L0_attn_Wv': _L0_attn_in['Wv'], 'L0_attn_Wo': _L0_attn_in['Wo'], 'L0_attn_Wg': _L0_attn_in['Wg'], 'L0_ffn_router_w': _L0_ffn_in['router_w'], 'L0_ffn_router_b': _L0_ffn_in['router_b'], 'L0_ffn_expert_w': _L0_ffn_in['expert_w'], 'L0_ffn_expert_b': _L0_ffn_in['expert_b']}

def reference(x, L0_tok_conv_w, L0_tok_conv_b, L0_tok_score_w, L0_tok_embed_w, L0_tok_embed_b, L0_attn_Wq, L0_attn_Wk, L0_attn_Wv, L0_attn_Wo, L0_attn_Wg, L0_ffn_router_w, L0_ffn_router_b, L0_ffn_expert_w, L0_ffn_expert_b):
    import jax
    import jax.numpy as jnp

    def _L0_tok_ref(img, conv_w, conv_b, score_w, embed_w, embed_b):
        import jax, jax.numpy as jnp
        import numpy as np
        from jax import lax
        B, C, H, W = (8, 3, 128, 128)
        S, D = (196, 192)
        logits = lax.conv_general_dilated(img, conv_w, window_strides=(1, 1), padding='SAME', dimension_numbers=('NCHW', 'OIHW', 'NCHW'))
        logits = logits + conv_b[None, :, None, None]
        labels = jnp.argmax(logits, axis=1)
        seg_ids = jnp.arange(S)
        masks = (labels[:, None] == seg_ids[None, :, None, None]).astype(img.dtype)
        masked = img[:, None] * masks[:, :, None]
        score = jnp.einsum('bschw,c->bshw', masked, score_w)
        attn = jax.nn.softmax(score.reshape(score.shape[0], S, -1), axis=-1)
        attn = attn.reshape(score.shape)
        pooled = jnp.einsum('bschw,bshw->bsc', masked, attn)
        feats = pooled @ embed_w + embed_b
        present = (jnp.sum(masks, axis=(2, 3)) > 0).astype(feats.dtype)
        return feats * present[..., None]

    def _L0_attn_ref(x, Wq, Wk, Wv, Wo, Wg):
        import jax, jax.numpy as jnp
        import numpy as np
        B, T, DM = (4, 512, 192)
        H, D = (4, 64)
        DIM = H * D

        def _feature_map(x):
            return jax.nn.elu(x) + 1.0
        Bx, Tx, _ = x.shape
        q = _feature_map((x @ Wq).reshape(Bx, Tx, H, D))
        k = _feature_map((x @ Wk).reshape(Bx, Tx, H, D))
        v = (x @ Wv).reshape(Bx, Tx, H, D)
        qT = q.transpose(1, 0, 2, 3)
        kT = k.transpose(1, 0, 2, 3)
        vT = v.transpose(1, 0, 2, 3)
        S0 = jnp.zeros((Bx, H, D, D), x.dtype)
        z0 = jnp.zeros((Bx, H, D), x.dtype)

        def step(carry, inp):
            S, z = carry
            qi, ki, vi = inp
            S = S + ki[..., :, None] * vi[..., None, :]
            z = z + ki
            num = jnp.einsum('bhd,bhde->bhe', qi, S)
            den = jnp.maximum(jnp.sum(qi * z, axis=-1), 1e-06)
            return ((S, z), num / den[..., None])
        (_, _), outT = jax.lax.scan(step, (S0, z0), (qT, kT, vT))
        out = outT.transpose(1, 0, 2, 3).reshape(Bx, Tx, DIM)
        gate = jax.nn.sigmoid(x @ Wg)
        return out @ Wo * gate

    def _L0_ffn_ref(x, router_w, router_b, expert_w, expert_b):
        import jax, jax.numpy as jnp
        import numpy as np
        B, S, H = (4, 2048, 192)
        E, K = (8, 2)
        scores = jnp.einsum('bsh,eh->bse', x, router_w) + router_b
        probs = jax.nn.softmax(scores, axis=-1)
        top_probs, expert_ids = jax.lax.top_k(probs, K)
        y = jnp.einsum('bsh,edh->bsed', x, expert_w) + expert_b
        out_k = jnp.take_along_axis(y, expert_ids[..., None], axis=2)
        w = top_probs / (jnp.sum(top_probs, axis=-1, keepdims=True) + 1e-09)
        out = jnp.einsum('bsk,bskh->bsh', w, out_k)
        return out
    h = _L0_tok_ref(x, L0_tok_conv_w, L0_tok_conv_b, L0_tok_score_w, L0_tok_embed_w, L0_tok_embed_b)
    h = h + _L0_attn_ref(_layernorm(h, axis=-1), L0_attn_Wq, L0_attn_Wk, L0_attn_Wv, L0_attn_Wo, L0_attn_Wg)
    h = h + _L0_ffn_ref(_layernorm(h, axis=-1), L0_ffn_router_w, L0_ffn_router_b, L0_ffn_expert_w, L0_ffn_expert_b)
    return h

_drawn_inputs = setup_inputs


def setup_inputs(seed=0):
    import zlib

    import numpy as np

    out = dict(_drawn_inputs(seed))
    spreads = {}
    factors = {'L0_attn_Wq': 8.0, 'L0_attn_Wk': 5.216}
    for name, (base, spread) in spreads.items():
        noise = np.random.default_rng([zlib.crc32(name.encode()), seed]).standard_normal(out[name].shape)
        drawn = base * np.exp(spread * noise) if base else spread * noise
        out[name] = jnp.asarray(drawn.astype(out[name].dtype))
    for name, factor in factors.items():
        out[name] = (out[name] * factor).astype(out[name].dtype)
    return out
```

```python
from contextlib import ExitStack

import numpy as np
import concourse.bass as bass
from concourse import mybir

ALU = mybir.AluOpType
ACT = mybir.ActivationFunctionType
AX = mybir.AxisListType
RED = bass.bass_isa.ReduceOp
F32 = mybir.dt.float32
BF16 = mybir.dt.bfloat16

P = 128
H = W = 128
C = 3
S = 196
SC = S // 2
PW = W + 2
TAPS = 9
PLANES = 12
KROWS = TAPS * PLANES + 2
LOGIT_SCALE = 2.0 ** 64
ONES_PAIR = float(np.array([0x3F803F80], np.uint32).view(np.float32)[0])
NF = 13
NSUM = 5

GROUPS = [4] * 31 + [2, 2]
STARTS = [sum(GROUPS[:k]) for k in range(len(GROUPS))]
NG = len(GROUPS)
SLOTS = 3
RING = 11
assert NG % SLOTS == 0 and NG % RING == 0


def constants():
    keep = np.ones((KROWS, 2), np.float32)
    q3 = np.array([(r % PLANES) >= 9 for r in range(TAPS * PLANES)] + [False, True])
    keep[:, 0] = ~q3
    keep[:, 1] = q3
    sel = np.zeros((P, NSUM), np.float32)
    for r in range(P):
        if r % 32 < 12:
            sel[r, (r % 32) % 4] = 1.0
        elif r % 32 == 12:
            sel[r, 4] = 1.0
    tri = np.triu(np.ones((SC, SC), np.float32))
    return keep, sel, np.eye(P, dtype=np.float32), tri


class Steps:

    def __init__(self, eng, sem, base=0):
        self.eng, self.sem, self.value = eng, sem, base

    def __call__(self, ins):
        ins.then_inc(self.sem, 1)
        self.value = self.value + 1
        self.eng.wait_ge(self.sem, self.value)


def dve_picks(k):
    return 2 if k % 4 == 1 and GROUPS[k] == 4 else 0


def banks(k):
    return (GROUPS[k] + 1) // 2


def made(k, bank):
    by_dve = [bool(dve_picks(j)) and c == 1 for j in range(NG) for c in range(banks(j))]
    at = sum(banks(j) for j in range(k)) + bank
    return by_dve[at], sum(1 for j in range(at + 1) if by_dve[j] == by_dve[at])


N_DVE = sum(1 for k in range(NG) if dve_picks(k))
N_ACT = sum(banks(k) for k in range(NG)) - N_DVE


def segment_sums(nc, ctx, x, conv_w108, conv_b, score_w, keep_d, sel_d, pad_d, stats, negmax, psum):
    B = x.shape[0]
    x_v = x.rearrange("b c h w -> b h c w")

    def sb(name, shape, dt):
        return ctx.enter_context(nc.sbuf_tensor(name, shape, dt))

    def sem(name):
        return ctx.enter_context(nc.semaphore(name))

    patches = sb("patches", [P, 2, H * PW], BF16)
    xin = sb("xin", [P, 2, C, W], F32)
    xs = sb("xs", [P, 2, 9, PW], BF16)
    xres = sb("xres", [P, C, W], F32)
    score = sb("score", [P, 2, W], F32)
    term = sb("term", [P, C, W], F32)
    feat = sb("feat", [P, 2, 4, W], F32)
    fres = sb("fres", [P, 4, W], F32)
    fs = sb("fs", [P, 2, 32, W], BF16)
    pmax = sb("pmax", [P, 2], F32)
    imax = sb("imax", [P, 2], F32)
    negm = sb("negm", [P, 2], F32)
    onehot = sb("onehot", [P, RING, 4, S], BF16)
    negmx = sb("negmx", [P, RING, 4], F32)
    scw = sb("scw", [P, C], F32)
    wrep = sb("wrep", [P, S], F32)
    wsc = sb("wsc", [P, S], F32)
    wres = sb("wres", [P, S], F32)
    w1 = sb("w1", [P, S], BF16)
    w2 = sb("w2", [P, S], BF16)
    w3 = sb("w3", [P, S], BF16)
    w3k = sb("w3k", [P, S], BF16)
    wA = sb("wA", [P, S], BF16)
    wB = sb("wB", [P, S], BF16)
    keep = sb("keep", [P, 2], F32)
    sel = sb("sel", [P, NSUM], F32)
    accs = sb("accs", [P, 2, S], F32)
    zero = sb("zero", [P, 1], F32)
    zrow = sb("zrow", [PLANES, PW], BF16)
    logits = [psum[:, 2 * s:2 * s + 2] for s in range(SLOTS)]
    acc = psum[:, 6:8]
    tot = acc[:, :, 256:256 + 2 * NSUM]

    consts_in = sem("consts_in")
    borders_out = sem("borders_out")
    pool_init_done = sem("pool_init")
    ones_rows = sem("ones_rows")
    conv_w_ready = sem("conv_w_ready")
    dve_steps = sem("dve_steps")
    x_in = [sem(f"x_in{p}") for p in range(2)]
    split_done = sem("split_done")
    planes_out = [sem(f"planes_out{p}") for p in range(2)]
    patches_in = [sem(f"patches_in{p}") for p in range(2)]
    pool_steps = sem("pool_steps")
    score_ready = sem("score_ready")
    pmax_ready = sem("pmax_ready")
    imax_ready = sem("imax_ready")
    negm_ready = sem("negm_ready")
    negm_kept = sem("negm_kept")
    e_ready = sem("e_ready")
    feats_ready = sem("feats_ready")
    logits_ready = sem("logits_ready")
    max_ready = sem("max_ready")
    hot_act = sem("hot_act")
    hot_dve = sem("hot_dve")
    image_done = sem("image_done")
    acc_copied = sem("acc_copied")
    tot_ready = sem("tot_ready")
    tot_copied = sem("tot_copied")

    x_v = x.rearrange("b c h w -> b h c w")

    pad_v = [pad_d[p, :, 0:(H + 2) * PW].rearrange("q (h w) -> h q w", w=PW)[1:H + 1] for p in range(2)]

    def pairs(eng, pair):
        n = B // 2
        pair(0, True, n == 1)
        if n > 2:
            with eng.Fori(1, n - 1) as i:
                pair(i, False, False)
        if n > 1:
            pair(n - 1, False, True)

    def sp_load_x(sp, n, par, first):
        if not first:
            sp.wait_ge(feats_ready, 2 * n + par - 1)
        sp.dma_start(xin[:, par], x_v[2 * n + par]).then_inc(x_in[par], 16)

    def sp_patches(sp, n, par, first):
        sp.wait_ge(split_done, 2 * n + par + 1)
        sp.dma_start(pad_v[par][:, 0:9, :], xs[:, par]).then_inc(planes_out[par], 16)
        sp.dma_start(pad_v[par][:, 9:12, :], xs[:, par, 0:3]).then_inc(planes_out[par], 16)
        sp.wait_ge(planes_out[par], n * 32 + 32)
        if not first:
            sp.wait_ge(image_done, 2 * n + par - 1)
        for j in range(TAPS):
            off = (j // 3) * PW + j % 3
            sp.dma_start(patches[j * PLANES:(j + 1) * PLANES, par], pad_d[par, :, off:off + H * PW]).then_inc(patches_in[par], 16)

    def sp_constants(sp):
        sp.dma_start(wrep[0:KROWS - 2], conv_w108).then_inc(consts_in, 16)
        for r in (KROWS - 2, KROWS - 1):
            sp.dma_start(wrep[r:r + 1], conv_b.rearrange("(a s) -> a s", a=1)).then_inc(consts_in, 16)
        sp.dma_start(keep[0:KROWS], keep_d).then_inc(consts_in, 16)
        sp.dma_start(sel[:, :], sel_d).then_inc(consts_in, 16)
        sp.dma_start(scw[:, :], score_w.rearrange("(a c) -> a c", a=1).to_broadcast([P, C])).then_inc(consts_in, 16)
        sp_load_x(sp, 0, 0, True)

    def sp_program(sp):
        sp.wait_ge(pool_init_done, 1)
        for p in range(2):
            for r in (0, H + 1):
                sp.dma_start(pad_d[p, :, r * PW:(r + 1) * PW], zrow[:, :]).then_inc(borders_out, 16)
            tail = pad_d.shape[2] - (H + 2) * PW
            sp.dma_start(pad_d[p, :, (H + 2) * PW:], zrow[:, 0:tail]).then_inc(borders_out, 16)
        sp.wait_ge(borders_out, 96)
        sp.wait_ge(ones_rows, 1)
        sp_patches(sp, 0, 0, True)

        def pair(i, first, last):
            sp_load_x(sp, i, 1, first)
            if first:
                sp.wait_ge(ones_rows, 2)
            sp_patches(sp, i, 1, first)
            if not last:
                sp_load_x(sp, i + 1, 0, False)
                sp_patches(sp, i + 1, 0, False)

        pairs(sp, pair)

    POOL_STEPS = 9

    def zeros(m):
        return zero[:, 0:1].unsqueeze(2).to_broadcast([P, m, W])

    def pool_image(pool, n, par, first):
        b = 2 * n + par
        steps = [b * POOL_STEPS]

        def step(ins):
            ins.then_inc(pool_steps, 1)
            steps[0] = steps[0] + 1
            pool.wait_ge(pool_steps, steps[0])

        X = xin[:, par]
        x1, x2, x3 = (xs[:, par, 3 * q:3 * q + 3, 1:W + 1] for q in range(3))
        pool.wait_ge(x_in[par], n * 16 + 16)
        if not first:
            pool.wait_ge(e_ready, b - 1)
        step(pool.tensor_tensor(term[:, :, :], X, scw[:, :].unsqueeze(2).to_broadcast([P, C, W]), ALU.mult))
        step(pool.tensor_tensor(term[:, 0], term[:, 0], term[:, 1], ALU.add))
        pool.tensor_tensor(score[:, par], term[:, 0], term[:, 2], ALU.add).then_inc(score_ready, 1)
        if not first:
            pool.wait_ge(patches_in[par], n * (16 * TAPS))
        step(pool.tensor_tensor(x1, X, zeros(C), ALU.add))
        step(pool.tensor_tensor(xres[:, :, :], X, x1, ALU.subtract))
        step(pool.tensor_tensor(x2, xres[:, :, :], zeros(C), ALU.add))
        pool.wait_ge(pmax_ready, b + 1)
        pool.tensor_tensor(x3, xres[:, :, :], x2, ALU.subtract).then_inc(split_done, 1)
        pool.partition_all_reduce(imax[:, par:par + 1], pmax[:, par:par + 1], P, RED.max).then_inc(imax_ready, 1)
        f1, f2, f3 = (fs[:, par, 4 * q:4 * q + 4] for q in range(3))
        pool.wait_ge(split_done, b + 1)
        pool.wait_ge(e_ready, b + 1)
        step(pool.tensor_tensor(feat[:, par, 1:4], X, feat[:, par, 0:1].to_broadcast([P, C, W]), ALU.mult))
        if not first:
            pool.wait_ge(image_done, b - 1)
        step(pool.tensor_tensor(f1, feat[:, par], zeros(4), ALU.add))
        step(pool.tensor_tensor(fres[:, :, :], feat[:, par], f1, ALU.subtract))
        step(pool.tensor_tensor(f2, fres[:, :, :], zeros(4), ALU.add))
        pool.tensor_tensor(f3, fres[:, :, :], f2, ALU.subtract).then_inc(feats_ready, 1)
        pool.wait_ge(feats_ready, b + 1)
        assert first is None or not isinstance(b, int) or steps[0] == (b + 1) * POOL_STEPS, steps

    def pool_init(pool):
        pool.memset(zrow[:, :], 0.0).then_inc(pool_init_done, 1)
        pool.memset(zero[:, :], 0.0).then_inc(pool_init_done, 1)
        for p in range(2):
            pool.memset(xs[:, p], 0.0).then_inc(pool_init_done, 1)
            pool.memset(fs[:, p, 12:13], 1.0).then_inc(pool_init_done, 1)
            pool.memset(fs[:, p, 13:32], 0.0).then_inc(pool_init_done, 1)

    def pool_program(pool):
        pool.wait_ge(consts_in, 96)
        pool.wait_ge(pool_init_done, 8)
        pool_image(pool, 0, 0, True)
        pool.memset(patches[96:P, 1].bitcast(F32), ONES_PAIR).then_inc(ones_rows, 1)
        pool.wait_ge(ones_rows, 2)

        def pair(i, first, last):
            pool_image(pool, i, 1, first)
            if not last:
                pool_image(pool, i + 1, 0, False)

        pairs(pool, pair)

    LAG = SLOTS
    tap_rows = [patches[:, p].rearrange("q (h w) -> q h w", w=PW) for p in range(2)]

    def wait_hot(pe, b, k, bank):
        by_dve, count = made(k, bank)
        if by_dve:
            pe.wait_ge(hot_dve, b * N_DVE + count)
        else:
            pe.wait_ge(hot_act, b * N_ACT + count)

    def pe_logits(pe, b, par, k, first):
        for t in range(GROUPS[k]):
            if t % 2 == 0 and not first:
                before = (b, k - SLOTS) if k >= SLOTS else (b - 1, k - SLOTS + NG)
                if t // 2 < banks(before[1]):
                    wait_hot(pe, *before, t // 2)
            w = STARTS[k] + t
            out = logits[k % SLOTS][:, t // 2, (t % 2) * S:(t % 2 + 1) * S]
            pe.matmul(out, tap_rows[par][:, :, w], wA[:, :], start=True, stop=False, skip_group_check=True)
            mm = pe.matmul(out, tap_rows[par][:, :, w], wB[:, :], start=False, stop=True, skip_group_check=True)
        mm.then_inc(logits_ready, 1)

    def pe_sums(pe, b, par, k):
        for t in range(GROUPS[k]):
            if t % 2 == 0:
                wait_hot(pe, b, k, t // 2)
            w = STARTS[k] + t
            q = w % 4
            mm = pe.matmul(acc[32 * q:32 * q + 32, par, 0:S], fs[:, par, :, w], onehot[:, k % RING, t],
                           start=(w < 4), stop=(w >= W - 4), skip_group_check=True)
        if k == NG - 1:
            mm.then_inc(image_done, 1)

    def pe_total(pe, b_done, par):
        pe.wait_ge(acc_copied, b_done + 1)
        for c in range(2):
            mm = pe.matmul(tot[0:SC, par, NSUM * c:NSUM * (c + 1)], accs[:, par, SC * c:SC * (c + 1)], sel[:, :],
                           start=True, stop=True)
        mm.then_inc(tot_ready, 1)

    def pe_image(pe, n, par, first, last):
        b = 2 * n + par
        for k in range(NG):
            if k + LAG < NG:
                pe_logits(pe, b, par, k + LAG, False)
            elif not last:
                if k + LAG == NG:
                    nn = n + 1 if par else n
                    pe.wait_ge(patches_in[1 - par], nn * (16 * TAPS) + 16 * TAPS)
                pe_logits(pe, b + 1, 1 - par, k + LAG - NG, False)
            if k == 0:
                pe.wait_ge(feats_ready, b + 1)
                if not first:
                    pe.wait_ge(tot_copied, b - 1)
            pe_sums(pe, b, par, k)
            if k == TOTAL_AT and not (first and par == 0):
                pe_total(pe, b - 1, 1 - par)

    COPY_AT, TOTAL_AT, KEEP_AT = 2, 6, 9

    def pe_program(pe):
        pe.wait_ge(conv_w_ready, 1)
        pe.wait_ge(patches_in[0], 16 * TAPS)
        for k in range(LAG):
            pe_logits(pe, 0, 0, k, True)

        def pair(i, first, last):
            pe_image(pe, i, 0, first, False)
            pe_image(pe, i, 1, first, last)

        pairs(pe, pair)
        pe_total(pe, B - 1, 1)

    def dve_pmax(dve, b, par):
        dve.wait_ge(score_ready, b + 1)
        dve.tensor_reduce(pmax[:, par:par + 1], score[:, par], AX.X, ALU.max).then_inc(pmax_ready, 1)

    def dve_negm(dve, b, par, first):
        dve.wait_ge(imax_ready, b + 1)
        if not first:
            dve.wait_ge(e_ready, b - 1)
        dve.tensor_scalar(negm[:, par:par + 1], imax[:, par:par + 1], -1.0, 0.0, ALU.mult, ALU.min).then_inc(negm_ready, 1)
        dve.tensor_scalar(negmax[:, bass.ds(b, 1)], imax[:, par:par + 1], -1.0, 0.0, ALU.mult, ALU.min).then_inc(negm_kept, 1)

    def dve_copy_acc(dve, b_done, par):
        dve.wait_ge(image_done, b_done + 1)
        dve.tensor_copy(accs[:, par], acc[:, par, 0:S]).then_inc(acc_copied, 1)

    def dve_keep(dve, b_done, par):
        dve.wait_ge(tot_ready, b_done + 1)
        dve.tensor_copy(stats[0:SC, bass.ds(b_done, 1), :], tot[0:SC, par:par + 1, :]).then_inc(tot_copied, 1)

    def dve_image(dve, n, par, first, last):
        b = 2 * n + par
        for k in range(NG):
            dve.wait_ge(logits_ready, b * NG + k + 1)
            m = GROUPS[k]
            src = logits[k % SLOTS][:, 0:banks(k), 0:2 * S].rearrange("p b (t s) -> p b t s", t=2)
            dst = negmx[:, k % RING, 0:m].rearrange("p (b t) -> p b t", b=banks(k))
            dve.tensor_reduce(dst, src, AX.X, ALU.max, negate=True).then_inc(max_ready, 1)
            if k and dve_picks(k - 1):
                dve.wait_ge(max_ready, b * NG + k)
                dve.scalar_tensor_tensor(
                    out=onehot[:, (k - 1) % RING, 2:4], in0=logits[(k - 1) % SLOTS][:, 1, 0:2 * S].rearrange("p (t s) -> p t s", t=2),
                    scalar=-1.0, in1=negmx[:, (k - 1) % RING, 2:4].unsqueeze(2).to_broadcast([P, 2, S]),
                    op0=ALU.mult, op1=ALU.is_equal).then_inc(hot_dve, 1)
            if not last and k == 0:
                dve_pmax(dve, b + 1, 1 - par)
            if not last and k == 4:
                dve_negm(dve, b + 1, 1 - par, first and par == 0)
            if not (first and par == 0) and k == COPY_AT:
                dve_copy_acc(dve, b - 1, 1 - par)
            if not (first and par == 0) and k == KEEP_AT:
                dve_keep(dve, b - 1, 1 - par)

    def dve_program(dve):
        steps = [0]

        def step(ins):
            ins.then_inc(dve_steps, 1)
            steps[0] += 1
            dve.wait_ge(dve_steps, steps[0])

        dve.memset(patches[96:P, 0].bitcast(F32), ONES_PAIR).then_inc(ones_rows, 1)
        step(dve.memset(wA[96:P], 0.0))
        step(dve.memset(wB[96:P], 0.0))
        K = KROWS
        dve.wait_ge(consts_in, 96)
        step(dve.tensor_scalar(wsc[0:K], wrep[0:K], LOGIT_SCALE, None, ALU.mult))
        step(dve.tensor_copy(w1[0:K], wsc[0:K]))
        step(dve.tensor_tensor(wres[0:K], wsc[0:K], w1[0:K], ALU.subtract))
        step(dve.tensor_copy(w2[0:K], wres[0:K]))
        step(dve.tensor_tensor(w3[0:K], wres[0:K], w2[0:K], ALU.subtract))
        step(dve.tensor_scalar(w3k[0:K], w3[0:K], keep[0:K, 1:2], None, ALU.mult))
        step(dve.scalar_tensor_tensor(out=wA[0:K], in0=w1[0:K], scalar=keep[0:K, 0:1], in1=w3k[0:K], op0=ALU.mult, op1=ALU.add))
        dve.tensor_scalar(wB[0:K], w2[0:K], keep[0:K, 0:1], None, ALU.mult).then_inc(conv_w_ready, 1)
        dve_pmax(dve, 0, 0)
        dve_negm(dve, 0, 0, True)

        def pair(i, first, last):
            dve_image(dve, i, 0, first, False)
            dve_image(dve, i, 1, first, last)

        pairs(dve, pair)
        dve_copy_acc(dve, B - 1, 1)
        dve_keep(dve, B - 1, 1)
        return steps

    def act_e(act, b, par):
        act.wait_ge(negm_ready, b + 1)
        act.activation(feat[:, par, 0], score[:, par], ACT.Exp, bias=negm[:, par:par + 1]).then_inc(e_ready, 1)

    def act_image(act, n, par, last):
        b = 2 * n + par
        for k in range(NG):
            act.wait_ge(max_ready, b * NG + k + 1)
            n = GROUPS[k] - dve_picks(k)
            for t in range(n):
                hot = act.activation(onehot[:, k % RING, t], logits[k % SLOTS][:, t // 2, (t % 2) * S:(t % 2 + 1) * S],
                                     ACT.Exp, bias=negmx[:, k % RING, t:t + 1])
                if t % 2 == 1:
                    hot.then_inc(hot_act, 1)
            if not last and k == 8:
                act_e(act, b + 1, 1 - par)

    def act_program(act):
        act.preload_act_table(ACT.Exp)
        act_e(act, 0, 0)

        def pair(i, first, last):
            act_image(act, i, 0, False)
            act_image(act, i, 1, last)

        pairs(act, pair)

    return dict(sp_constants=sp_constants, pool_init=pool_init, sp=sp_program, pool=pool_program, pe=pe_program, dve=dve_program, act=act_program,
                slab=patches[:, :, :].rearrange("p a n -> p (a n)").bitcast(F32), sems=dict(tot_copied=tot_copied, negm_kept=negm_kept, dve_steps=dve_steps))


DIM = 192
HEADS, HD = 4, 64
EXPERTS = 8
KC = DIM // 2
CROWS = P
NTOK = H * W
LN_EPS = 1e-5
DEN_MIN = 1e-6
TOP_EPS = 1e-9


def layer(nc, ctx, B, wd, out_d, stats, negmax, identity_d, tri_d, psum, slab, stats_kept):
    def sb(name, shape, dt=F32):
        return ctx.enter_context(nc.sbuf_tensor(name, shape, dt))

    def sem(name):
        return ctx.enter_context(nc.semaphore(name))

    ident = sb("ident", [P, P])
    tri = sb("tri", [P, SC])
    e4 = sb("e4", [4, DIM])
    e4s = sb("e4s", [4, 2])
    ec = sb("ec", [4, DIM])
    ecT = sb("ecT", [KC, 2, 4])
    ecP = sb("ecP", [KC, 2, 16])
    ones = sb("ones", [P, SC])
    gram = sb("gram", [SC, 16])
    wqk = sb("wqk", [KC, 2, 2 * HEADS * HD])
    wg = sb("wg", [KC, 2, DIM])
    wv = sb("wv", [KC, 2, HEADS * HD])
    wo = sb("wo", [HD, HEADS, DIM])
    avT = sb("avT", [HD, HEADS, 16])
    mqk = sb("mqk", [CROWS, 2 * HEADS * HD])
    mout = sb("mout", [CROWS, 3 * DIM])
    wrt = sb("wrt", [P, 2, EXPERTS])
    wff = sb("wff", [P, 2, EXPERTS * DIM])

    slab_at = [0]

    def in_slab(rows, shape):
        n = int(np.prod(shape))
        v = slab[0:rows, slab_at[0]:slab_at[0] + n]
        slab_at[0] += n
        assert slab_at[0] <= slab.shape[1], slab_at
        names = [f"d{j}" for j in range(len(shape))]
        if len(shape) > 1:
            v = v.rearrange(f"p ({' '.join(names)}) -> p {' '.join(names)}", **dict(zip(names[1:], shape[1:])))
        return v

    enm = in_slab(SC, [B])
    zf = [in_slab(SC, [B, 2]) for j in range(4)]
    var = in_slab(SC, [B, 2])
    mhalf = sb("mhalf", [SC, 2])
    eps = sb("eps", [SC, 2])
    uz = in_slab(SC, [B, 2, 8])
    ct = sb("ct", [SC, 2, 2, CROWS])
    cT1 = in_slab(CROWS, [S])
    cT2 = in_slab(CROWS, [S])
    expx = in_slab(P, [2, 2 * S])
    relx = in_slab(P, [2, 2 * S])
    qk = in_slab(P, [2, 2 * S])
    aT = in_slab(SC, [HEADS, 3 * SC])
    den = sb("den", [SC, 2, HEADS])
    rden = sb("rden", [SC, 2, HEADS])
    th = in_slab(SC, [2, DIM])
    gated = in_slab(SC, [2, DIM])
    h1 = in_slab(SC, [2, 2, DIM])
    bns = sb("bns", [SC, 2, 6])
    mv = sb("mv", [SC, 2, 2])
    vare = sb("vare", [SC, 2])
    rstd = sb("rstd", [SC, 2])
    x2 = in_slab(SC, [2, DIM])
    xT = sb("xT", [P, 2, 2, S])
    rs = sb("rs", [SC, 2, 16])
    rd = sb("rd", [SC, 2, 10])
    re = sb("re", [SC, 2, 10])
    rsum = sb("rsum", [SC, 2])
    rtop = sb("rtop", [SC, 2])
    rnorm = sb("rnorm", [SC, 2])
    rinv = sb("rinv", [SC, 2])
    rmask = sb("rmask", [SC, 2, EXPERTS])
    rw = sb("rw", [SC, 2, EXPERTS])
    wt = sb("wt", [SC, 2, 2, EXPERTS])
    mixa = in_slab(SC, [2, 2, DIM])
    mixb = in_slab(SC, [2, 2, DIM])
    outb = in_slab(SC, [2, 2, DIM])

    names = ("weights_in init_done pads_done pe_prep prep_copied act_prep uz_steps uz_ready pow_ready "
             "placed t1_done ct1_ready qk_done er_ready elu_ready at_done at_copied masked n_done y_steps y_ready "
             "t2_done ct2_ready o_done th_ready gated_ready h1_ready var_steps var_ready rstd_steps rstd_ready x2_ready t3_done xt_ready "
             "r_done r_steps rd_ready re_ready w_ready ff_done mixed out_ready stored0 stored1").split()
    sm = {n: sem(n) for n in names}

    def wait(eng, name, value):
        if isinstance(value, int) and value <= 0:
            return
        eng.wait_ge(sm[name], value)

    A, Q, F = psum[:, 0:4], psum[:, 4:6], psum[:, 6:8]

    def sp_weights(sp):
        n = [0]

        def load(dst, src):
            sp.dma_start(dst, src).then_inc(sm["weights_in"], 16)
            n[0] += 1

        load(ident[:, :], identity_d)
        load(tri[0:SC, :], tri_d)
        load(e4[0:3, :], wd["embed_w"])
        load(e4[3:4, :], wd["embed_b"].rearrange("(a d) -> a d", a=1))
        for j, m in enumerate(("Wq", "Wk")):
            load(wqk[:, :, j * 256:(j + 1) * 256], wd[m].rearrange("(c p) n -> p c n", p=KC))
        load(wg[:, :, :], wd["Wg"].rearrange("(c p) n -> p c n", p=KC))
        load(wv[:, :, :], wd["Wv"].rearrange("(c p) n -> p c n", p=KC))
        load(wo[:, :, :], wd["Wo"].rearrange("(h p) n -> p h n", p=HD))
        load(wrt[0:KC], wd["router_wT"].rearrange("(c p) e -> p c e", p=KC))
        wait(sp, "pads_done", 2)
        load(wrt[KC:KC + 1, 0, :], wd["router_b"].rearrange("(a d) -> a d", a=1))
        for c in range(2):
            load(wff[0:KC, c].rearrange("p (e d) -> p e d", e=EXPERTS), wd["expert_wT"][:, c * KC:(c + 1) * KC, :].rearrange("e p d -> p e d"))
        load(wff[KC:KC + 1, 0, :], wd["expert_b"].rearrange("e d -> (e d)").rearrange("(a n) -> a n", a=1))
        assert n[0] == N_LOADS, n

    N_LOADS = 14

    def pool_init(pool):
        for t in (ct[:, :, :, :], mqk[:, :], mout[:, :], avT[:, :, :]):
            pool.memset(t, 0.0).then_inc(sm["init_done"], 1)
        wait(pool, "init_done", 4)
        pool.memset(wrt[KC:P], 0.0).then_inc(sm["pads_done"], 1)
        pool.memset(wff[KC:P], 0.0).then_inc(sm["pads_done"], 1)
        wait(pool, "pads_done", 2)
        pool.memset(ones[:, :], 1.0).then_inc(sm["init_done"], 1)
        pool.memset(mhalf[:, :], -0.5).then_inc(sm["init_done"], 1)
        wait(pool, "init_done", 6)
        pool.memset(eps[:, :], LN_EPS).then_inc(sm["init_done"], 1)
        wait(pool, "init_done", 7)
        pool.memset(xT[KC:P], 1.0).then_inc(sm["init_done"], 1)
        wait(pool, "init_done", 8)
        pool.memset(ct[:, :, :, 4:5], 1.0).then_inc(sm["init_done"], 1)
        wait(pool, "init_done", 9)

    def pe_prep(pe):
        wait(pe, "weights_in", 16 * N_LOADS)
        wait(pe, "init_done", 9)
        wait(pe, "prep_copied", 1)
        for c in range(2):
            mm = pe.transpose(A[0:KC, 0, 4 * c:4 * c + 4], ec[:, c * KC:(c + 1) * KC], ident[0:4, 0:4])
        mm.then_inc(sm["pe_prep"], 1)
        wait(pe, "prep_copied", 3)
        for c in range(2):
            mm = pe.matmul(A[0:SC, 1, 0:16], ones[0:KC, 0:SC], ecP[:, c], start=(c == 0), stop=(c == 1))
        mm.then_inc(sm["pe_prep"], 1)
        for c in range(2):
            pe.matmul(A[0:4, 2, 0:512], ecT[:, c], wqk[:, c], start=(c == 0), stop=(c == 1))
        for c in range(2):
            pe.matmul(A[0:4, 3, 0:DIM], ecT[:, c], wg[:, c], start=(c == 0), stop=(c == 1))
        for h in range(HEADS):
            for c in range(2):
                mm = pe.matmul(Q[0:HD, 0, 4 * h:4 * h + 4], wv[:, c, h * HD:(h + 1) * HD], ecT[:, c],
                               start=(c == 0), stop=(c == 1))
        mm.then_inc(sm["pe_prep"], 1)
        wait(pe, "prep_copied", 4)
        for h in range(HEADS):
            mm = pe.matmul(Q[0:16, 1, 0:DIM], avT[:, h], wo[:, h], start=(h == 0), stop=(h == HEADS - 1))
        mm.then_inc(sm["pe_prep"], 1)

    def act_prep(act):
        act.wait_ge(stats_kept[0], B)
        act.activation(enm[:, :], negmax[0:SC, :], ACT.Exp).then_inc(sm["act_prep"], 1)
        wait(act, "uz_steps", N_VAR)
        act.activation(zf[0][:, :, :], var[:, :, :], ACT.Sqrt).then_inc(sm["act_prep"], 1)
        act.preload_act_table(ACT.Exp)

    N_VAR = 33

    def dve_prep(dve):
        wait(dve, "weights_in", 16 * N_LOADS)
        wait(dve, "init_done", 9)
        dve.wait_ge(stats_kept[0], B)
        dve.wait_ge(stats_kept[1], B)
        st = Steps(dve, sm["uz_steps"])
        st(dve.tensor_reduce(e4s[:, 0:1], e4[:, :], AX.X, ALU.add))
        st(dve.tensor_scalar(e4s[:, 1:2], e4s[:, 0:1], -1.0 / DIM, None, ALU.mult))
        dve.tensor_scalar(ec[:, :], e4[:, :], e4s[:, 1:2], None, ALU.add).then_inc(sm["prep_copied"], 1)
        wait(dve, "pe_prep", 1)
        dve.tensor_copy(ecT[:, :, :], A[0:KC, 0, 0:8].rearrange("p (c j) -> p c j", c=2)).then_inc(sm["prep_copied"], 1)
        wait(dve, "prep_copied", 2)
        for c in range(2):
            rows = ecT[:, c].unsqueeze(2).to_broadcast([KC, 4, 4])
            cols = ecT[:, c].unsqueeze(1).to_broadcast([KC, 4, 4])
            ins = dve.scalar_tensor_tensor(out=ecP[:, c].rearrange("p (i j) -> p i j", i=4), in0=rows, scalar=1.0 / DIM,
                                           in1=cols, op0=ALU.mult, op1=ALU.mult)
        ins.then_inc(sm["prep_copied"], 1)
        wait(dve, "pe_prep", 2)
        st(dve.tensor_copy(gram[:, :], A[0:SC, 1, 0:16]))
        wait(dve, "pe_prep", 3)
        st(dve.tensor_copy(mqk[0:4, :], A[0:4, 2, 0:512]))
        st(dve.tensor_copy(mout[0:4, DIM:2 * DIM], A[0:4, 3, 0:DIM]))
        for h in range(HEADS):
            ins = dve.tensor_copy(avT[:, h, 4 * h:4 * h + 4], Q[0:HD, 0, 4 * h:4 * h + 4])
        ins.then_inc(sm["prep_copied"], 1)
        wait(dve, "act_prep", 1)
        sv = stats[0:SC].rearrange("p b (c k) -> p b c k", c=2)
        st(dve.tensor_scalar(var[:, :, :], sv[:, :, :, 4], -1.0, float(NTOK), ALU.mult, ALU.add))
        st(dve.tensor_tensor(var[:, :, :], var[:, :, :], enm[:, :].unsqueeze(2).to_broadcast([SC, B, 2]), ALU.mult))
        st(dve.tensor_tensor(var[:, :, :], var[:, :, :], sv[:, :, :, 0], ALU.add))
        st(dve.reciprocal(var[:, :, :], var[:, :, :]))
        for j in range(3):
            dve.tensor_tensor(uz[:, :, :, 4 + j], sv[:, :, :, 1 + j], var[:, :, :], ALU.mult)
        st(dve.tensor_scalar(uz[:, :, :, 7], sv[:, :, :, 4], 0.0, None, ALU.is_gt))
        z = [uz[:, :, :, 4 + j] for j in range(4)]
        for i in range(4):
            t = zf[i][:, :, :]
            st(dve.tensor_scalar(t, z[0], gram[:, 4 * i:4 * i + 1], None, ALU.mult))
            for j in range(1, 4):
                st(dve.scalar_tensor_tensor(out=t, in0=z[j], scalar=gram[:, 4 * i + j:4 * i + j + 1], in1=t,
                                            op0=ALU.mult, op1=ALU.add))
            st(dve.tensor_tensor(t, t, z[i], ALU.mult))
        st(dve.tensor_tensor(zf[0][:, :, :], zf[0][:, :, :], zf[1][:, :, :], ALU.add))
        st(dve.tensor_tensor(zf[2][:, :, :], zf[2][:, :, :], zf[3][:, :, :], ALU.add))
        st(dve.scalar_tensor_tensor(out=var[:, :, :], in0=zf[0][:, :, :], scalar=LN_EPS, in1=zf[2][:, :, :],
                                    op0=ALU.add, op1=ALU.add))
        assert st.value == N_VAR, st.value
        wait(dve, "act_prep", 2)
        st(dve.reciprocal(zf[1][:, :, :], zf[0][:, :, :]))
        st(dve.tensor_tensor(zf[2][:, :, :], zf[1][:, :, :], zf[1][:, :, :], ALU.mult))
        st(dve.scalar_tensor_tensor(out=zf[3][:, :, :], in0=zf[2][:, :, :], scalar=-0.5, in1=var[:, :, :],
                                    op0=ALU.mult, op1=ALU.mult))
        st(dve.scalar_tensor_tensor(out=zf[2][:, :, :], in0=zf[3][:, :, :], scalar=1.5, in1=zf[1][:, :, :],
                                    op0=ALU.add, op1=ALU.mult))
        for j in range(4):
            last = dve.tensor_tensor(uz[:, :, :, j], z[j], zf[2][:, :, :], ALU.mult)
        last.then_inc(sm["uz_ready"], 1)
        wait(dve, "pe_prep", 4)
        dve.tensor_copy(mout[64:80, 0:DIM], Q[0:16, 1, 0:DIM]).then_inc(sm["uz_ready"], 1)
        dve.tensor_copy(mout[32:36, 2 * DIM:3 * DIM], e4[:, :]).then_inc(sm["uz_ready"], 1)

    def pool_place(pool, b, par):
        wait(pool, "t2_done", b - 1)
        wait(pool, "uz_ready", 1)
        pool.tensor_copy(ct[:, par].rearrange("p c (g k) -> p c g k", k=16)[:, :, 0:4:2, 0:4],
                         uz[:, bass.ds(b, 1)].rearrange("p b c (g k) -> p (b c) g k", k=4)).then_inc(sm["placed"], 1)

    def pe_t1(pe, b, par):
        wait(pe, "placed", b + 1)
        wait(pe, "y_ready", b)
        for c in range(2):
            mm = pe.transpose(A[0:CROWS, 0, SC * c:SC * (c + 1)], ct[:, par, c], ident[0:SC, 0:SC])
        mm.then_inc(sm["t1_done"], 1)

    def act_ct1(act, b, par):
        wait(act, "t1_done", b + 1)
        act.copy(cT1[:, :], A[0:CROWS, 0, 0:S]).then_inc(sm["ct1_ready"], 1)

    def pe_qk(pe, b, hp):
        wait(pe, "ct1_ready", b + 1)
        for j in range(2):
            mm = pe.matmul(A[:, 2 + hp, j * S:(j + 1) * S], mqk[:, 256 * j + 128 * hp:256 * j + 128 * (hp + 1)], cT1[:, :],
                           start=True, stop=True)
        mm.then_inc(sm["qk_done"], 1)

    def act_elu(act, b, hp):
        wait(act, "qk_done", 2 * b + hp + 1)
        act.activation(expx[:, hp], A[:, 2 + hp, 0:2 * S], ACT.Exp)
        act.activation(relx[:, hp], A[:, 2 + hp, 0:2 * S], ACT.Relu).then_inc(sm["er_ready"], 1)

    def dve_elu(dve, b, hp):
        wait(dve, "er_ready", 2 * b + hp + 1)
        dve.scalar_tensor_tensor(out=qk[:, hp], in0=expx[:, hp], scalar=1.0, in1=relx[:, hp],
                                 op0=ALU.min, op1=ALU.add).then_inc(sm["elu_ready"], 1)

    def pe_scores(pe, b, hp):
        wait(pe, "elu_ready", 2 * b + hp + 1)
        for r in range(2):
            rows = slice(HD * r, HD * (r + 1))
            q, k = qk[rows, hp, 0:S], qk[rows, hp, S:2 * S]
            pe.matmul(A[0:SC, 2 * hp + r, 0:S], k[:, 0:SC], q, start=True, stop=True)
            mm = pe.matmul(A[0:SC, 2 * hp + r, S:S + SC], k[:, SC:S], q[:, SC:S], start=True, stop=True)
        mm.then_inc(sm["at_done"], 1)

    def act_scores(act, b, hp):
        wait(act, "at_done", 2 * b + hp + 1)
        act.copy(aT[:, 2 * hp:2 * hp + 2], A[0:SC, 2 * hp:2 * hp + 2, 0:3 * SC]).then_inc(sm["at_copied"], 1)

    def pool_mask(pool, b, hp):
        wait(pool, "at_copied", 2 * b + hp + 1)
        for r in range(2):
            v = aT[:, 2 * hp + r].rearrange("p (g i) -> p g i", g=3)[:, 0:3:2]
            ins = pool.tensor_tensor(v, v, tri[0:SC].unsqueeze(1).to_broadcast([SC, 2, SC]), ALU.mult)
        ins.then_inc(sm["masked"], 1)

    def pe_sums2(pe, b, par, hp):
        wait(pe, "masked", 2 * b + hp + 1)
        for h in (2 * hp, 2 * hp + 1):
            o = [A[0:SC, 0, 20 * c + 5 * h:20 * c + 5 * h + 5] for c in range(2)]
            pe.matmul(o[0], aT[:, h, 0:SC], ct[:, par, 0, 0:5], start=True, stop=True)
            pe.matmul(o[1], aT[:, h, SC:2 * SC], ct[:, par, 0, 0:5], start=True, stop=False)
            mm = pe.matmul(o[1], aT[:, h, 2 * SC:3 * SC], ct[:, par, 1, 0:5], start=False, stop=True)
        mm.then_inc(sm["n_done"], 1)

    def dve_y(dve, b, par):
        wait(dve, "n_done", 2 * b + 2)
        st = Steps(dve, sm["y_steps"], 2 * b)
        num = A[0:SC, 0, 0:40].rearrange("p (c h k) -> p c h k", c=2, h=HEADS)
        st(dve.tensor_scalar(den[:, :, :], num[:, :, :, 4], DEN_MIN, None, ALU.max))
        st(dve.reciprocal(rden[:, :, :], den[:, :, :]))
        out = ct[:, par, :, 64:80].rearrange("p c (h k) -> p c h k", h=HEADS)
        dve.tensor_tensor(out, num[:, :, :, 0:4], rden[:, :, :].unsqueeze(3).to_broadcast([SC, 2, HEADS, 4]),
                          ALU.mult).then_inc(sm["y_ready"], 1)

    def pe_t2(pe, b, par):
        wait(pe, "y_ready", b + 1)
        wait(pe, "xt_ready", b)
        for c in range(2):
            mm = pe.transpose(Q[0:CROWS, 0, SC * c:SC * (c + 1)], ct[:, par, c], ident[0:SC, 0:SC])
        mm.then_inc(sm["t2_done"], 1)

    def act_ct2(act, b):
        wait(act, "t2_done", b + 1)
        act.copy(cT2[:, :], Q[0:CROWS, 0, 0:S]).then_inc(sm["ct2_ready"], 1)

    def pe_out(pe, b, c):
        wait(pe, "ct2_ready", b + 1)
        if c == 0:
            wait(pe, "rd_ready", b)
            for cc in range(2):
                pe.matmul(Q[0:SC, 1, DIM * cc:DIM * (cc + 1)], cT2[:, SC * cc:SC * (cc + 1)], mout[:, 2 * DIM:3 * DIM],
                          start=True, stop=True)
        else:
            wait(pe, "gated_ready", 2 * b + 1)
        pe.matmul(Q[0:SC, 0, 0:2 * DIM], cT2[:, SC * c:SC * (c + 1)], mout[:, 0:2 * DIM],
                  start=True, stop=True).then_inc(sm["o_done"], 1)

    def act_gate(act, b, c):
        wait(act, "o_done", 2 * b + c + 1)
        act.activation(th[:, c], Q[0:SC, 0, DIM:2 * DIM], ACT.Tanh, scale=0.5).then_inc(sm["th_ready"], 1)

    def dve_h1(dve, b, par, c):
        wait(dve, "th_ready", 2 * b + c + 1)
        dve.scalar_tensor_tensor(out=gated[:, c], in0=th[:, c], scalar=1.0, in1=Q[0:SC, 0, 0:DIM],
                                 op0=ALU.add, op1=ALU.mult).then_inc(sm["gated_ready"], 1)
        wait(dve, "gated_ready", 2 * b + c + 1)
        dve.scalar_tensor_tensor(out=h1[:, par, c], in0=gated[:, c], scalar=0.5, in1=Q[0:SC, 1, DIM * c:DIM * (c + 1)],
                                 op0=ALU.mult, op1=ALU.add).then_inc(sm["h1_ready"], 1)

    def dve_stats2(dve, b, par):
        wait(dve, "h1_ready", 2 * b + 2)
        for c in range(2):
            dve.bn_stats(bns[:, c], h1[:, par, c]).then_inc(sm["var_steps"], 1)
        wait(dve, "var_steps", 2 * b + 2)

    def dve_aggregate(dve, b):
        for c in range(2):
            ins = dve.bn_aggr(mv[:, c], bns[:, c])
        ins.then_inc(sm["var_ready"], 1)

    def pool_rstd(pool, b):
        wait(pool, "var_ready", b + 1)
        pool.tensor_tensor(vare[:, :], mv[:, :, 1], eps[:, :], ALU.add).then_inc(sm["rstd_steps"], 1)
        wait(pool, "rstd_steps", b + 1)
        pool.tensor_tensor(rstd[:, :], vare[:, :], mhalf[:, :], ALU.pow).then_inc(sm["rstd_ready"], 1)

    def dve_x2(dve, b, par):
        wait(dve, "rstd_ready", b + 1)
        for c in range(2):
            ins = dve.tensor_scalar(x2[:, c], h1[:, par, c], mv[:, c, 0:1], rstd[:, c:c + 1], ALU.subtract, ALU.mult)
        ins.then_inc(sm["x2_ready"], 1)

    def pe_t3(pe, b):
        wait(pe, "x2_ready", b + 1)
        for kc in range(2):
            for c in range(2):
                mm = pe.transpose(Q[0:KC, 0, S * kc + SC * c:S * kc + SC * (c + 1)], x2[:, c, KC * kc:KC * (kc + 1)],
                                  ident[0:SC, 0:SC])
        mm.then_inc(sm["t3_done"], 1)

    def act_xt(act, b, par):
        wait(act, "t3_done", b + 1)
        wait(act, "ff_done", 8 * (b - 1))
        act.copy(xT[0:KC, par].rearrange("p k s -> p (k s)"), Q[0:KC, 0, 0:2 * S]).then_inc(sm["xt_ready"], 1)

    def rows_of(t, par, kc, c):
        return t[:, par, kc, SC * c:SC * (c + 1)]

    def pe_router(pe, b, par):
        wait(pe, "xt_ready", b + 1)
        for c in range(2):
            for kc in range(2):
                mm = pe.matmul(Q[0:SC, 1, EXPERTS * c:EXPERTS * (c + 1)], rows_of(xT, par, kc, c), wrt[:, kc],
                               start=(kc == 0), stop=(kc == 1))
        mm.then_inc(sm["r_done"], 1)

    def dve_router1(dve, b):
        wait(dve, "r_done", b + 1)
        dve.tensor_copy(rs[:, :, 0:EXPERTS], Q[0:SC, 1, 0:2 * EXPERTS].rearrange("p (c e) -> p c e", c=2)).then_inc(sm["r_steps"], 1)
        for c in range(2):
            ins = dve.max(rs[:, c, 8:16], Q[0:SC, 1, EXPERTS * c:EXPERTS * (c + 1)])
        ins.then_inc(sm["r_steps"], 1)
        wait(dve, "r_steps", b * N_RSTEPS + 2)
        dve.tensor_tensor(rd[:, :, :], rs[:, :, 0:10], rs[:, :, 8:9].to_broadcast([SC, 2, 10]), ALU.subtract)\
           .then_inc(sm["rd_ready"], 1)

    def act_router(act, b):
        wait(act, "rd_ready", b + 1)
        act.activation(re[:, :, :], rd[:, :, :], ACT.Exp).then_inc(sm["re_ready"], 1)

    N_RSTEPS = 5

    def dve_router2(dve, b, par):
        wait(dve, "re_ready", b + 1)
        st = Steps(dve, sm["r_steps"], b * N_RSTEPS + 2)
        dve.tensor_reduce(rsum[:, :], re[:, :, 0:EXPERTS], AX.X, ALU.add)
        dve.tensor_tensor(rmask[:, :, :], rd[:, :, 0:EXPERTS], rd[:, :, 9:10].to_broadcast([SC, 2, EXPERTS]), ALU.is_ge)
        st(dve.tensor_tensor(rtop[:, :], re[:, :, 8], re[:, :, 9], ALU.add))
        dve.tensor_tensor(rw[:, :, :], rmask[:, :, :], re[:, :, 0:EXPERTS], ALU.mult)
        st(dve.scalar_tensor_tensor(out=rnorm[:, :], in0=rsum[:, :], scalar=TOP_EPS, in1=rtop[:, :], op0=ALU.mult, op1=ALU.add))
        st(dve.reciprocal(rinv[:, :], rnorm[:, :]))
        dve.tensor_tensor(wt[:, par], rw[:, :, :], rinv[:, :].unsqueeze(2).to_broadcast([SC, 2, EXPERTS]), ALU.mult)\
           .then_inc(sm["w_ready"], 1)

    def pe_experts(pe, b, par, n):
        c, pair = n // 4, n % 4
        wait(pe, "mixed", 16 * b + 2 * n - 2)
        for kc in range(2):
            mm = pe.matmul(F[0:SC, n % 2, 0:2 * DIM], rows_of(xT, par, kc, c), wff[:, kc, 2 * DIM * pair:2 * DIM * (pair + 1)],
                           start=(kc == 0), stop=(kc == 1))
        mm.then_inc(sm["ff_done"], 1)

    def dve_mix(dve, b, par, n):
        c, pair = n // 4, n % 4
        wait(dve, "ff_done", 8 * b + n + 1)
        if n == 0:
            wait(dve, "w_ready", b + 1)
            wait(dve, "out_ready", 2 * b - 2)
        for r, mix in ((0, mixa), (1, mixb)):
            e = 2 * pair + r
            y, w = F[0:SC, n % 2, DIM * r:DIM * (r + 1)], wt[:, par, c, e:e + 1]
            if pair:
                wait(dve, "mixed", 16 * b + 2 * n - 1 + r)
            if pair == 0 and r == 1:
                ins = dve.tensor_scalar(mix[:, par, c], y, w, None, ALU.mult)
            else:
                ins = dve.scalar_tensor_tensor(out=mix[:, par, c], in0=y, scalar=w, in1=(mix if pair else h1)[:, par, c],
                                               op0=ALU.mult, op1=ALU.add)
            ins.then_inc(sm["mixed"], 1)

    def pool_out(pool, b, par, c):
        wait(pool, "mixed", 16 * b + 8 * (c + 1))
        wait(pool, f"stored{par}", 8 * (b - par))
        pool.tensor_tensor(outb[:, par, c], mixa[:, par, c], mixb[:, par, c], ALU.add).then_inc(sm["out_ready"], 1)

    def sp_store(sp, b, par):
        wait(sp, "out_ready", 2 * b + 2)
        sp.dma_start(out_d[b].rearrange("(c p) d -> p c d", c=2), outb[:, par]).then_inc(sm[f"stored{par}"], 16)

    def pe_step(pe, s, par, one, two, three):
        a, p1 = s, par
        q, p2 = s - 1, 1 - par
        f, p3 = s - 2, par
        if one:
            pe_t1(pe, a, p1)
        if two:
            pe_t2(pe, q, p2)
        if three:
            pe_experts(pe, f, p3, 0)
        if one:
            pe_qk(pe, a, 0)
            pe_qk(pe, a, 1)
        if two:
            pe_out(pe, q, 0)
        if three:
            pe_experts(pe, f, p3, 1)
        if one:
            pe_scores(pe, a, 0)
        if three:
            pe_experts(pe, f, p3, 2)
        if two:
            pe_out(pe, q, 1)
        if one:
            pe_scores(pe, a, 1)
        if three:
            pe_experts(pe, f, p3, 3)
            pe_experts(pe, f, p3, 4)
        if one:
            pe_sums2(pe, a, p1, 0)
        if three:
            pe_experts(pe, f, p3, 5)
        if two:
            pe_t3(pe, q)
        if three:
            pe_experts(pe, f, p3, 6)
        if one:
            pe_sums2(pe, a, p1, 1)
        if two:
            pe_router(pe, q, p2)
        if three:
            pe_experts(pe, f, p3, 7)

    def act_step(act, s, par, one, two, three):
        a, q, p2 = s, s - 1, 1 - par
        if one:
            act_ct1(act, a, par)
        if two:
            act_ct2(act, q)
        if one:
            act_elu(act, a, 0)
            act_elu(act, a, 1)
        if two:
            act_gate(act, q, 0)
        if one:
            act_scores(act, a, 0)
        if two:
            act_gate(act, q, 1)
        if one:
            act_scores(act, a, 1)
        if two:
            act_xt(act, q, p2)
            act_router(act, q)

    def dve_step(dve, s, par, one, two, three):
        a, q, f = s, s - 1, s - 2
        p2 = 1 - par
        if three:
            dve_mix(dve, f, par, 0)
        if one:
            dve_elu(dve, a, 0)
            dve_elu(dve, a, 1)
        if three:
            dve_mix(dve, f, par, 1)
        if two:
            dve_h1(dve, q, p2, 0)
        if three:
            dve_mix(dve, f, par, 2)
        if two:
            dve_h1(dve, q, p2, 1)
            dve_stats2(dve, q, p2)
        if three:
            dve_mix(dve, f, par, 3)
        if two:
            dve_aggregate(dve, q)
            dve_x2(dve, q, p2)
        if three:
            dve_mix(dve, f, par, 4)
            dve_mix(dve, f, par, 5)
        if one:
            dve_y(dve, a, par)
        if two:
            dve_router1(dve, q)
        if three:
            dve_mix(dve, f, par, 6)
        if two:
            dve_router2(dve, q, p2)
        if three:
            dve_mix(dve, f, par, 7)

    def pool_step(pool, s, par, one, two, three):
        a, q, f = s, s - 1, s - 2
        if one:
            pool_place(pool, a, par)
            pool_mask(pool, a, 0)
        if two:
            pool_rstd(pool, q)
        if three:
            pool_out(pool, f, par, 0)
        if one:
            pool_mask(pool, a, 1)
        if three:
            pool_out(pool, f, par, 1)

    def sp_step(sp, s, par, one, two, three):
        if three:
            sp_store(sp, s - 2, par)

    def steps(eng, step):
        step(eng, 0, 0, True, False, False)
        step(eng, 1, 1, True, True, False)
        step(eng, 2, 0, True, True, True)
        step(eng, 3, 1, True, True, True)
        if B > 4:
            with eng.Fori(2, B // 2) as i:
                step(eng, 2 * i, 0, True, True, True)
                step(eng, 2 * i + 1, 1, True, True, True)
        step(eng, B, 0, False, True, True)
        step(eng, B + 1, 1, False, False, True)

    def sp_program(sp):
        steps(sp, sp_step)
        for par in range(2):
            wait(sp, f"stored{par}", 8 * B)

    def pool_program(pool):
        wait(pool, "uz_ready", 1)
        steps(pool, pool_step)

    def pe_program(pe):
        pe_prep(pe)
        wait(pe, "uz_ready", 3)
        steps(pe, pe_step)

    def act_program(act):
        act_prep(act)
        steps(act, act_step)

    def dve_program(dve):
        dve_prep(dve)
        steps(dve, dve_step)

    return dict(sp_weights=sp_weights, pool_init=pool_init, sp=sp_program, pool=pool_program, pe=pe_program,
                act=act_program, dve=dve_program)


def build(nc, a, out_d, n_images):
    B = n_images
    with ExitStack() as ctx:
        psum = ctx.enter_context(nc.psum_tensor("psum", [P, 8, 512], F32))[:, :, :]
        stats = ctx.enter_context(nc.sbuf_tensor("stats", [P, B, 2 * NSUM], F32))
        negmax = ctx.enter_context(nc.sbuf_tensor("negmax", [P, B], F32))
        pad_d = nc.dram_tensor("planes_pad", [2, PLANES, (H + 2) * PW + 60], BF16).ap()
        first = segment_sums(nc, ctx, a["x"], a["conv_w108"], a["conv_b"], a["score_w"], a["keep"], a["sel"], pad_d,
                             stats, negmax, psum)
        sems = first["sems"]
        second = layer(nc, ctx, B, a, out_d, stats, negmax, a["ident"], a["tri"], psum,
                       first["slab"], (sems["tot_copied"], sems["negm_kept"]))
        block = ctx.enter_context(nc.Block())

        @block.sync
        def _(sp):
            first["sp_constants"](sp)
            second["sp_weights"](sp)
            first["sp"](sp)
            second["sp"](sp)

        @block.gpsimd
        def _(pool):
            first["pool_init"](pool)
            second["pool_init"](pool)
            first["pool"](pool)
            second["pool"](pool)

        @block.tensor
        def _(pe):
            first["pe"](pe)
            second["pe"](pe)

        @block.scalar
        def _(act):
            first["act"](act)
            second["act"](act)

        @block.vector
        def _(dve):
            first["dve"](dve)
            second["dve"](dve)


def kernel(**inputs):
    import numpy as _np
    import concourse.bacc as _bacc
    from concourse import mybir as _mybir
    from concourse.bass_utils import run_bass_kernel_spmd as _run

    given = {k: _np.asarray(v) for k, v in inputs.items()}
    arrays = layout(given)
    n_images = given["x"].shape[0]
    nc = _bacc.Bacc("TRN2", target_bir_lowering=False, num_devices=1)
    aps = {n: nc.dram_tensor(f"in_{n}", v.shape, _mybir.dt.from_np(v.dtype), kind="ExternalInput").ap()
           for n, v in arrays.items()}
    out_d = nc.dram_tensor("out", (n_images, S, DIM), _mybir.dt.float32, kind="ExternalOutput").ap()
    build(nc, aps, out_d, n_images)
    r = _run(nc, [{f"in_{n}": v for n, v in arrays.items()}], core_ids=[0])
    return r.results[0]["out"]


def layout(given):
    keep, sel, ident, tri = constants()
    w = given["L0_tok_conv_w"].transpose(2, 3, 1, 0).reshape(TAPS, 1, C, S)
    arrays = {
        "x": given["x"],
        "conv_w108": np.broadcast_to(w, (TAPS, PLANES // C, C, S)).reshape(TAPS * PLANES, S),
        "conv_b": given["L0_tok_conv_b"],
        "score_w": given["L0_tok_score_w"],
        "embed_w": given["L0_tok_embed_w"],
        "embed_b": given["L0_tok_embed_b"],
        "Wq": given["L0_attn_Wq"], "Wk": given["L0_attn_Wk"], "Wv": given["L0_attn_Wv"],
        "Wo": given["L0_attn_Wo"], "Wg": given["L0_attn_Wg"],
        "router_wT": given["L0_ffn_router_w"].T,
        "router_b": given["L0_ffn_router_b"],
        "expert_wT": given["L0_ffn_expert_w"].transpose(0, 2, 1),
        "expert_b": given["L0_ffn_expert_b"],
        "keep": keep, "sel": sel, "ident": ident, "tri": tri,
    }
    return {n: np.ascontiguousarray(v) for n, v in arrays.items()}
```

```python
from contextlib import ExitStack

import numpy as np
import concourse.bass as bass
from concourse import mybir

ALU = mybir.AluOpType
ACT = mybir.ActivationFunctionType
AX = mybir.AxisListType
RED = bass.bass_isa.ReduceOp
F32 = mybir.dt.float32
BF16 = mybir.dt.bfloat16

P = 128
H = W = 128
C = 3
S = 196
SC = S // 2
PW = W + 2
TAPS = 9
PLANES = 12
KROWS = TAPS * PLANES + 2
LOGIT_SCALE = 2.0 ** 64
ONES_PAIR = float(np.array([0x3F803F80], np.uint32).view(np.float32)[0])
NF = 13
NSUM = 5
CROWS = P

GROUPS = [2] * (W // 2)
STARTS = [sum(GROUPS[:k]) for k in range(len(GROUPS))]
NG = len(GROUPS)
SLOTS = 4
RING = 16
assert NG % SLOTS == 0 and NG % RING == 0

PE_AT = dict(total=5, t1=1, qk=(5, 7), scores=(12, 14, 16, 18), sums=26, t2=33, out=(37, 44), t3=55, router=59,
             experts=(8, 10, 15, 17, 21, 23, 28, 30, 34, 36, 41, 43, 47, 49, 54, 56), prep=(12, 22, 34))
ACT_AT = dict(e=24, ct1=3, elu=(7, 10), scores=(14, 16, 18, 20), ct2=35, gate=(40, 46), xt=57, router=1)
DVE_AT = dict(copy=4, keep=11, pmax=14, negm=24, elu=(14, 17), y=34, h1=(46, 52), aggregate=54, x2=57, router1=2,
              router2=7, mix=(16, 23, 29, 36, 42, 49, 55, 62), prep=(8, 16, 28, 40))


def constants():
    keep = np.ones((KROWS, 2), np.float32)
    q3 = np.array([(r % PLANES) >= 9 for r in range(TAPS * PLANES)] + [False, True])
    keep[:, 0] = ~q3
    keep[:, 1] = q3
    sel = np.zeros((P, NSUM), np.float32)
    for r in range(P):
        if r % 32 < 12:
            sel[r, (r % 32) % 4] = 1.0
        elif r % 32 == 12:
            sel[r, 4] = 1.0
    tri = np.triu(np.ones((SC, SC), np.float32))
    return keep, sel, np.eye(P, dtype=np.float32), tri


class Steps:

    def __init__(self, eng, sem, base=0):
        self.eng, self.sem, self.value = eng, sem, base

    def __call__(self, ins):
        ins.then_inc(self.sem, 1)
        self.value = self.value + 1
        self.eng.wait_ge(self.sem, self.value)


def need(eng, sem, value):
    if isinstance(value, int) and value <= 0:
        return
    eng.wait_ge(sem, value)


def image(i, par, shift):
    return i + (par + shift) // 2, (par + shift) % 2


def by_dve(k):
    return k % 12 == 5


def made(k):
    return by_dve(k), sum(1 for j in range(k + 1) if by_dve(j) == by_dve(k))


N_DVE = sum(1 for k in range(NG) if by_dve(k))
N_ACT = NG - N_DVE
assert not by_dve(NG - 1)


def segment_sums(nc, ctx, x, conv_w108, conv_b, score_w, keep_d, sel_d, pad_d, psum, tot):
    B = x.shape[0]
    x_v = x.rearrange("b c h w -> b h c w")

    def sb(name, shape, dt):
        return ctx.enter_context(nc.sbuf_tensor(name, shape, dt))

    def sem(name):
        return ctx.enter_context(nc.semaphore(name))

    patches = sb("patches", [P, 2, H * PW], BF16)
    xin = sb("xin", [P, 2, C, W], F32)
    xs = sb("xs", [P, 2, 9, PW], BF16)
    xres = sb("xres", [P, C, W], F32)
    score = sb("score", [P, 2, W], F32)
    term = sb("term", [P, C, W], F32)
    feat = sb("feat", [P, 2, 4, W], F32)
    fres = sb("fres", [P, 4, W], F32)
    fs = sb("fs", [P, 2, 32, W], BF16)
    pmax = sb("pmax", [P, 2], F32)
    imax = sb("imax", [P, 2], F32)
    negm = sb("negm", [P, 2], F32)
    onehot = sb("onehot", [P, RING, 2, S], BF16)
    negmx = sb("negmx", [P, RING, 2], F32)
    scw = sb("scw", [P, C], F32)
    wrep = sb("wrep", [P, S], F32)
    wsc = sb("wsc", [P, S], F32)
    wres = sb("wres", [P, S], F32)
    w1 = sb("w1", [P, S], BF16)
    w2 = sb("w2", [P, S], BF16)
    w3 = sb("w3", [P, S], BF16)
    w3k = sb("w3k", [P, S], BF16)
    wA = sb("wA", [P, S], BF16)
    wB = sb("wB", [P, S], BF16)
    keep = sb("keep", [P, 2], F32)
    sel = sb("sel", [P, NSUM], F32)
    accs = sb("accs", [P, 2, S], F32)
    zero = sb("zero", [P, 1], F32)
    zrow = sb("zrow", [PLANES, PW], BF16)
    logits = [psum[:, s] for s in range(SLOTS)]
    acc = psum[:, SLOTS]
    enm = sb("enm", [SC, 2], F32)
    ct = sb("ct", [SC, 2, 2, CROWS], F32)
    sums = sb("sums", [SC, 2, 2 * NSUM], F32)

    consts_in = sem("consts_in")
    borders_out = sem("borders_out")
    pool_init_done = sem("pool_init")
    ones_rows = sem("ones_rows")
    conv_w_ready = sem("conv_w_ready")
    dve_steps = sem("dve_steps")
    x_in = [sem(f"x_in{p}") for p in range(2)]
    split_done = sem("split_done")
    planes_out = [sem(f"planes_out{p}") for p in range(2)]
    patches_in = [sem(f"patches_in{p}") for p in range(2)]
    pool_steps = sem("pool_steps")
    score_ready = sem("score_ready")
    pmax_ready = sem("pmax_ready")
    imax_ready = sem("imax_ready")
    negm_ready = sem("negm_ready")
    enm_ready = sem("enm_ready")
    placed = sem("placed")
    t2_done = sem("t2_done")
    e_ready = sem("e_ready")
    feats_ready = sem("feats_ready")
    logits_ready = sem("logits_ready")
    max_ready = sem("max_ready")
    hot_act = sem("hot_act")
    hot_dve = sem("hot_dve")
    image_done = sem("image_done")
    acc_copied = sem("acc_copied")
    tot_ready = sem("tot_ready")
    tot_copied = sem("tot_copied")

    x_v = x.rearrange("b c h w -> b h c w")

    pad_v = [pad_d[p, :, 0:(H + 2) * PW].rearrange("q (h w) -> h q w", w=PW)[1:H + 1] for p in range(2)]

    def sp_load_x(sp, n, par):
        need(sp, feats_ready, 2 * n + par - 1)
        sp.dma_start(xin[:, par], x_v[2 * n + par]).then_inc(x_in[par], 16)

    def sp_patches(sp, n, par):
        sp.wait_ge(split_done, 2 * n + par + 1)
        sp.dma_start(pad_v[par][:, 0:9, :], xs[:, par]).then_inc(planes_out[par], 16)
        sp.dma_start(pad_v[par][:, 9:12, :], xs[:, par, 0:3]).then_inc(planes_out[par], 16)
        sp.wait_ge(planes_out[par], n * 32 + 32)
        need(sp, image_done, 2 * n + par - 1)
        for j in range(TAPS):
            off = (j // 3) * PW + j % 3
            sp.dma_start(patches[j * PLANES:(j + 1) * PLANES, par], pad_d[par, :, off:off + H * PW]).then_inc(patches_in[par], 16)

    def sp_constants(sp):
        sp.dma_start(wrep[0:KROWS - 2], conv_w108).then_inc(consts_in, 16)
        for r in (KROWS - 2, KROWS - 1):
            sp.dma_start(wrep[r:r + 1], conv_b.rearrange("(a s) -> a s", a=1)).then_inc(consts_in, 16)
        sp.dma_start(keep[0:KROWS], keep_d).then_inc(consts_in, 16)
        sp.dma_start(sel[:, :], sel_d).then_inc(consts_in, 16)
        sp.dma_start(scw[:, :], score_w.rearrange("(a c) -> a c", a=1).to_broadcast([P, C])).then_inc(consts_in, 16)
        sp_load_x(sp, 0, 0)
        sp_load_x(sp, 0, 1)

    def sp_start(sp):
        sp.wait_ge(pool_init_done, 1)
        for p in range(2):
            for r in (0, H + 1):
                sp.dma_start(pad_d[p, :, r * PW:(r + 1) * PW], zrow[:, :]).then_inc(borders_out, 16)
            tail = pad_d.shape[2] - (H + 2) * PW
            sp.dma_start(pad_d[p, :, (H + 2) * PW:], zrow[:, 0:tail]).then_inc(borders_out, 16)
        sp.wait_ge(borders_out, 96)
        sp.wait_ge(ones_rows, 2)
        sp_patches(sp, 0, 0)

    POOL_STEPS = 9

    def zeros(m):
        return zero[:, 0:1].unsqueeze(2).to_broadcast([P, m, W])

    def pool_split(pool, n, par):
        b = 2 * n + par
        step = Steps(pool, pool_steps, b * POOL_STEPS)
        X = xin[:, par]
        x1, x2, x3 = (xs[:, par, 3 * q:3 * q + 3, 1:W + 1] for q in range(3))
        pool.wait_ge(x_in[par], n * 16 + 16)
        need(pool, e_ready, b - 1)
        step(pool.tensor_tensor(term[:, :, :], X, scw[:, :].unsqueeze(2).to_broadcast([P, C, W]), ALU.mult))
        step(pool.tensor_tensor(term[:, 0], term[:, 0], term[:, 1], ALU.add))
        pool.tensor_tensor(score[:, par], term[:, 0], term[:, 2], ALU.add).then_inc(score_ready, 1)
        need(pool, patches_in[par], n * (16 * TAPS))
        step(pool.tensor_tensor(x1, X, zeros(C), ALU.add))
        step(pool.tensor_tensor(xres[:, :, :], X, x1, ALU.subtract))
        step(pool.tensor_tensor(x2, xres[:, :, :], zeros(C), ALU.add))
        pool.wait_ge(pmax_ready, b + 1)
        pool.tensor_tensor(x3, xres[:, :, :], x2, ALU.subtract).then_inc(split_done, 1)
        pool.partition_all_reduce(imax[:, par:par + 1], pmax[:, par:par + 1], P, RED.max).then_inc(imax_ready, 1)

    def pool_features(pool, n, par):
        b = 2 * n + par
        step = Steps(pool, pool_steps, b * POOL_STEPS + 5)
        X = xin[:, par]
        f1, f2, f3 = (fs[:, par, 4 * q:4 * q + 4] for q in range(3))
        pool.wait_ge(split_done, b + 1)
        pool.wait_ge(e_ready, b + 1)
        step(pool.tensor_tensor(feat[:, par, 1:4], X, feat[:, par, 0:1].to_broadcast([P, C, W]), ALU.mult))
        need(pool, image_done, b - 1)
        step(pool.tensor_tensor(f1, feat[:, par], zeros(4), ALU.add))
        step(pool.tensor_tensor(fres[:, :, :], feat[:, par], f1, ALU.subtract))
        step(pool.tensor_tensor(f2, fres[:, :, :], zeros(4), ALU.add))
        pool.tensor_tensor(f3, fres[:, :, :], f2, ALU.subtract).then_inc(feats_ready, 1)
        pool.wait_ge(feats_ready, b + 1)

    def pool_init(pool):
        pool.memset(zrow[:, :], 0.0).then_inc(pool_init_done, 1)
        pool.memset(zero[:, :], 0.0).then_inc(pool_init_done, 1)
        for p in range(2):
            pool.memset(xs[:, p], 0.0).then_inc(pool_init_done, 1)
            pool.memset(fs[:, p, 12:13], 1.0).then_inc(pool_init_done, 1)
            pool.memset(fs[:, p, 13:32], 0.0).then_inc(pool_init_done, 1)
        pool.wait_ge(pool_init_done, 8)
        pool.memset(patches[96:P, 1].bitcast(F32), ONES_PAIR).then_inc(ones_rows, 1)
        pool.wait_ge(ones_rows, 2)
        pool.wait_ge(consts_in, 96)

    LAG = SLOTS
    FIRST_SUMS = 2
    tap_rows = [patches[:, p].rearrange("q (h w) -> q h w", w=PW) for p in range(2)]

    def wait_hot(pe, b, k):
        dve_made, count = made(k)
        if dve_made:
            need(pe, hot_dve, b * N_DVE + count)
        else:
            need(pe, hot_act, b * N_ACT + count)

    def pe_logits(pe, b, par, k):
        if k >= SLOTS:
            wait_hot(pe, b, k - SLOTS)
        else:
            wait_hot(pe, b - 1, k - SLOTS + NG)
        for t in range(GROUPS[k]):
            w = STARTS[k] + t
            out = logits[k % SLOTS][:, t * S:(t + 1) * S]
            pe.matmul(out, tap_rows[par][:, :, w], wA[:, :], start=True, stop=False, skip_group_check=True)
            mm = pe.matmul(out, tap_rows[par][:, :, w], wB[:, :], start=False, stop=True, skip_group_check=True)
        mm.then_inc(logits_ready, 1)

    def pe_sums(pe, b, par, k):
        if k == 0:
            pe.wait_ge(feats_ready, b + 1)
            need(pe, acc_copied, b)
        wait_hot(pe, b, k)
        for t in range(GROUPS[k]):
            w = STARTS[k] + t
            q = w % 4
            mm = pe.matmul(acc[32 * q:32 * q + 32, 0:S], fs[:, par, :, w], onehot[:, k % RING, t],
                           start=(w < 4), stop=(w >= W - 4), skip_group_check=True)
        if k == NG - 1:
            mm.then_inc(image_done, 1)

    def pe_total(pe, b, par):
        pe.wait_ge(acc_copied, b + 1)
        for c in range(2):
            mm = pe.matmul(tot[0:SC, NSUM * c:NSUM * (c + 1)], accs[:, par, SC * c:SC * (c + 1)], sel[:, :],
                           start=True, stop=True)
        mm.then_inc(tot_ready, 1)

    def pe_group(pe, i, par, k, more):
        b = 2 * i + par
        if k + LAG < NG:
            pe_logits(pe, b, par, k + LAG)
        elif more:
            n1, par1 = image(i, par, 1)
            if k + LAG == NG:
                pe.wait_ge(patches_in[par1], n1 * (16 * TAPS) + 16 * TAPS)
            pe_logits(pe, b + 1, par1, k + LAG - NG)
        if k >= FIRST_SUMS:
            for j in range(0 if k == FIRST_SUMS else k, k + 1):
                pe_sums(pe, b, par, j)

    def pe_start(pe):
        pe.wait_ge(conv_w_ready, 1)
        pe.wait_ge(patches_in[0], 16 * TAPS)
        for k in range(LAG):
            pe_logits(pe, 0, 0, k)

    def dve_pmax(dve, b, par):
        dve.wait_ge(score_ready, b + 1)
        dve.tensor_reduce(pmax[:, par:par + 1], score[:, par], AX.X, ALU.max).then_inc(pmax_ready, 1)

    def dve_negm(dve, b, par):
        dve.wait_ge(imax_ready, b + 1)
        need(dve, enm_ready, b - 1)
        dve.tensor_scalar(negm[:, par:par + 1], imax[:, par:par + 1], -1.0, 0.0, ALU.mult, ALU.min).then_inc(negm_ready, 1)

    def dve_copy_acc(dve, b, par):
        dve.wait_ge(image_done, b + 1)
        dve.tensor_copy(accs[:, par], acc[:, 0:S]).then_inc(acc_copied, 1)

    def dve_keep(dve, b, par):
        dve.wait_ge(tot_ready, b + 1)
        need(dve, placed, b - 1)
        dve.tensor_copy(sums[:, par], tot[0:SC, 0:2 * NSUM]).then_inc(tot_copied, 1)
        need(dve, t2_done, b - 1)
        dve.tensor_scalar(ct[:, par, :, 35], tot[0:SC, 0:2 * NSUM].rearrange("p (c k) -> p c k", c=2)[:, :, 4], 0.0, None,
                          ALU.is_gt).then_inc(tot_copied, 1)

    def dve_group(dve, b, k):
        dve.wait_ge(logits_ready, b * NG + k + 1)
        m = GROUPS[k]
        src = logits[k % SLOTS][:, 0:m * S].rearrange("p (t s) -> p t s", t=m)
        dve.tensor_reduce(negmx[:, k % RING, 0:m], src, AX.X, ALU.max, negate=True).then_inc(max_ready, 1)
        if k and by_dve(k - 1):
            dve.wait_ge(max_ready, b * NG + k)
            m = GROUPS[k - 1]
            dve.scalar_tensor_tensor(
                out=onehot[:, (k - 1) % RING, 0:m], in0=logits[(k - 1) % SLOTS][:, 0:m * S].rearrange("p (t s) -> p t s", t=m),
                scalar=-1.0, in1=negmx[:, (k - 1) % RING, 0:m].unsqueeze(2).to_broadcast([P, m, S]),
                op0=ALU.mult, op1=ALU.is_equal).then_inc(hot_dve, 1)

    def dve_start(dve):
        steps = [0]

        def step(ins):
            ins.then_inc(dve_steps, 1)
            steps[0] += 1
            dve.wait_ge(dve_steps, steps[0])

        dve.memset(patches[96:P, 0].bitcast(F32), ONES_PAIR).then_inc(ones_rows, 1)
        step(dve.memset(wA[96:P], 0.0))
        step(dve.memset(wB[96:P], 0.0))
        K = KROWS
        dve.wait_ge(consts_in, 96)
        step(dve.tensor_scalar(wsc[0:K], wrep[0:K], LOGIT_SCALE, None, ALU.mult))
        step(dve.tensor_copy(w1[0:K], wsc[0:K]))
        step(dve.tensor_tensor(wres[0:K], wsc[0:K], w1[0:K], ALU.subtract))
        step(dve.tensor_copy(w2[0:K], wres[0:K]))
        step(dve.tensor_tensor(w3[0:K], wres[0:K], w2[0:K], ALU.subtract))
        step(dve.tensor_scalar(w3k[0:K], w3[0:K], keep[0:K, 1:2], None, ALU.mult))
        step(dve.scalar_tensor_tensor(out=wA[0:K], in0=w1[0:K], scalar=keep[0:K, 0:1], in1=w3k[0:K], op0=ALU.mult, op1=ALU.add))
        dve.tensor_scalar(wB[0:K], w2[0:K], keep[0:K, 0:1], None, ALU.mult).then_inc(conv_w_ready, 1)
        dve_pmax(dve, 0, 0)
        dve_negm(dve, 0, 0)

    def act_e(act, b, par):
        act.wait_ge(negm_ready, b + 1)
        need(act, placed, b - 1)
        act.activation(feat[:, par, 0], score[:, par], ACT.Exp, bias=negm[:, par:par + 1]).then_inc(e_ready, 1)
        act.activation(enm[:, par:par + 1], negm[0:SC, par:par + 1], ACT.Exp).then_inc(enm_ready, 1)

    def act_group(act, b, k):
        if by_dve(k):
            return
        act.wait_ge(max_ready, b * NG + k + 1)
        for t in range(GROUPS[k]):
            hot = act.activation(onehot[:, k % RING, t], logits[k % SLOTS][:, t * S:(t + 1) * S],
                                 ACT.Exp, bias=negmx[:, k % RING, t:t + 1])
        hot.then_inc(hot_act, 1)

    return dict(sp_constants=sp_constants, sp_start=sp_start, sp_load_x=sp_load_x, sp_patches=sp_patches,
                pool_init=pool_init, pool_split=pool_split, pool_features=pool_features,
                pe_start=pe_start, pe_group=pe_group, pe_total=pe_total,
                dve_start=dve_start, dve_pmax=dve_pmax, dve_negm=dve_negm, dve_copy_acc=dve_copy_acc, dve_keep=dve_keep,
                dve_group=dve_group, act_e=act_e, act_group=act_group,
                enm=enm, sums=sums, tot_copied=tot_copied, enm_ready=enm_ready, placed=placed,
                t2_done=t2_done, ct=ct)


DIM = 192
HEADS, HD = 4, 64
EXPERTS = 8
KC = DIM // 2
NTOK = H * W
LN_EPS = 1e-5
DEN_MIN = 1e-6
TOP_EPS = 1e-9


def layer(nc, ctx, B, wd, out_d, identity_d, tri_d, psum, seg):
    def sb(name, shape, dt=F32):
        return ctx.enter_context(nc.sbuf_tensor(name, shape, dt))

    def sem(name):
        return ctx.enter_context(nc.semaphore(name))

    ident = sb("ident", [P, P])
    tri = sb("tri", [P, SC])
    e4 = sb("e4", [4, DIM])
    e4s = sb("e4s", [4, 2])
    ec = sb("ec", [4, DIM])
    ecT = sb("ecT", [KC, 2, 4])
    ecP = sb("ecP", [KC, 2, 16])
    ones = sb("ones", [P, SC])
    gram = sb("gram", [SC, 16])
    wqk = sb("wqk", [KC, 2, 2 * HEADS * HD])
    wg = sb("wg", [KC, 2, DIM])
    wv = sb("wv", [KC, 2, HEADS * HD])
    wo = sb("wo", [HD, HEADS, DIM])
    avT = sb("avT", [HD, HEADS, 16])
    mqk = sb("mqk", [CROWS, 2 * HEADS * HD])
    mout = sb("mout", [CROWS, 3 * DIM])
    wrt = sb("wrt", [P, 2, EXPERTS])
    wff = sb("wff", [P, 2, EXPERTS * DIM])

    den0 = sb("den0", [SC, 2])
    quad = sb("quad", [SC, 2, 16])
    zvar = sb("zvar", [SC, 2])
    zrstd = sb("zrstd", [SC, 2])
    ntok = sb("ntok", [SC, 2])
    minus1 = sb("minus1", [SC, 2])
    mhalf = sb("mhalf", [SC, 2])
    eps = sb("eps", [SC, 2])
    ct = seg["ct"]
    cT1 = sb("cT1", [CROWS, S])
    cT2 = sb("cT2", [CROWS, S])
    expx = sb("expx", [P, 2, 2 * S])
    relx = sb("relx", [P, 2, 2 * S])
    qk = sb("qk", [P, 2, 2 * S])
    aT = sb("aT", [SC, HEADS, 3 * SC])
    den = sb("den", [SC, 2, HEADS])
    rden = sb("rden", [SC, 2, HEADS])
    th = sb("th", [SC, 2, DIM])
    gated = sb("gated", [SC, 2, DIM])
    h1 = sb("h1", [SC, 2, 2, DIM])
    bns = sb("bns", [SC, 2, 6])
    mv = sb("mv", [SC, 2, 2])
    vare = sb("vare", [SC, 2])
    rstd = sb("rstd", [SC, 2])
    x2 = sb("x2", [SC, 2, DIM])
    xT = sb("xT", [P, 2, 2, S])
    rs = sb("rs", [SC, 2, 16])
    rd = sb("rd", [SC, 2, 10])
    re = sb("re", [SC, 2, 10])
    rsum = sb("rsum", [SC, 2])
    rtop = sb("rtop", [SC, 2])
    rnorm = sb("rnorm", [SC, 2])
    rinv = sb("rinv", [SC, 2])
    rmask = sb("rmask", [SC, 2, EXPERTS])
    rw = sb("rw", [SC, 2, EXPERTS])
    wt = sb("wt", [SC, 2, 2, EXPERTS])
    mixa = sb("mixa", [SC, 2, 2, DIM])
    mixb = sb("mixb", [SC, 2, 2, DIM])
    outb = sb("outb", [SC, 2, 2, DIM])

    names = ("weights_in init_done pads_done pe_prep prep_copied prep_steps mats_ready z_steps "
             "t1_done ct1_ready qk_done er_ready elu_ready at_done at_copied masked n_done y_steps y_ready "
             "ct2_ready o_done th_ready gated_ready h1_ready var_steps var_ready rstd_steps rstd_ready x2_ready t3_done xt_ready "
             "r_done r_steps rd_ready re_ready w_ready ff_done mixed out_ready stored0 stored1").split()
    sm = {n: sem(n) for n in names}
    for n in ("placed", "tot_copied", "t2_done"):
        sm[n] = seg[n]
    enm, sums = seg["enm"], seg["sums"]

    def wait(eng, name, value):
        if isinstance(value, int) and value <= 0:
            return
        eng.wait_ge(sm[name], value)

    G0, G1, F = psum[:, SLOTS + 1], psum[:, SLOTS + 2], psum[:, SLOTS + 3]

    def sp_weights(sp):
        n = [0]

        def load(dst, src):
            sp.dma_start(dst, src).then_inc(sm["weights_in"], 16)
            n[0] += 1

        load(ident[:, :], identity_d)
        load(tri[0:SC, :], tri_d)
        load(e4[0:3, :], wd["embed_w"])
        load(e4[3:4, :], wd["embed_b"].rearrange("(a d) -> a d", a=1))
        for j, m in enumerate(("Wq", "Wk")):
            load(wqk[:, :, j * 256:(j + 1) * 256], wd[m].rearrange("(c p) n -> p c n", p=KC))
        load(wg[:, :, :], wd["Wg"].rearrange("(c p) n -> p c n", p=KC))
        load(wv[:, :, :], wd["Wv"].rearrange("(c p) n -> p c n", p=KC))
        load(wo[:, :, :], wd["Wo"].rearrange("(h p) n -> p h n", p=HD))
        load(wrt[0:KC], wd["router_wT"].rearrange("(c p) e -> p c e", p=KC))
        wait(sp, "pads_done", 2)
        load(wrt[KC:KC + 1, 0, :], wd["router_b"].rearrange("(a d) -> a d", a=1))
        for c in range(2):
            load(wff[0:KC, c].rearrange("p (e d) -> p e d", e=EXPERTS), wd["expert_wT"][:, c * KC:(c + 1) * KC, :].rearrange("e p d -> p e d"))
        load(wff[KC:KC + 1, 0, :], wd["expert_b"].rearrange("e d -> (e d)").rearrange("(a n) -> a n", a=1))
        assert n[0] == N_LOADS, n

    N_LOADS = 14

    def pool_init(pool):
        for t in (ct[:, :, :, :], mqk[:, :], mout[:, :], avT[:, :, :]):
            pool.memset(t, 0.0).then_inc(sm["init_done"], 1)
        wait(pool, "init_done", 4)
        pool.memset(wrt[KC:P], 0.0).then_inc(sm["pads_done"], 1)
        pool.memset(wff[KC:P], 0.0).then_inc(sm["pads_done"], 1)
        wait(pool, "pads_done", 2)
        pool.memset(ones[:, :], 1.0).then_inc(sm["init_done"], 1)
        pool.memset(mhalf[:, :], -0.5).then_inc(sm["init_done"], 1)
        wait(pool, "init_done", 6)
        pool.memset(eps[:, :], LN_EPS).then_inc(sm["init_done"], 1)
        wait(pool, "init_done", 7)
        pool.memset(xT[KC:P], 1.0).then_inc(sm["init_done"], 1)
        wait(pool, "init_done", 8)
        pool.memset(ct[:, :, :, 4:5], 1.0).then_inc(sm["init_done"], 1)
        wait(pool, "init_done", 9)
        pool.memset(ntok[:, :], float(NTOK)).then_inc(sm["init_done"], 1)
        pool.memset(minus1[:, :], -1.0).then_inc(sm["init_done"], 1)
        wait(pool, "init_done", 11)

    def pe_prep(pe, n):
        if n == 0:
            wait(pe, "weights_in", 16 * N_LOADS)
            wait(pe, "init_done", 11)
            wait(pe, "prep_copied", 1)
            for c in range(2):
                mm = pe.transpose(G0[0:KC, 4 * c:4 * c + 4], ec[:, c * KC:(c + 1) * KC], ident[0:4, 0:4])
            mm.then_inc(sm["pe_prep"], 1)
        if n == 1:
            wait(pe, "prep_copied", 3)
            for c in range(2):
                pe.matmul(G1[0:SC, 0:16], ones[0:KC, 0:SC], ecP[:, c], start=(c == 0), stop=(c == 1))
            for c in range(2):
                pe.matmul(F[0:4, 0:512], ecT[:, c], wqk[:, c], start=(c == 0), stop=(c == 1))
            for c in range(2):
                pe.matmul(G0[0:4, 0:DIM], ecT[:, c], wg[:, c], start=(c == 0), stop=(c == 1))
            for h in range(HEADS):
                for c in range(2):
                    mm = pe.matmul(G1[0:HD, 32 + 4 * h:36 + 4 * h], wv[:, c, h * HD:(h + 1) * HD], ecT[:, c],
                                   start=(c == 0), stop=(c == 1))
            mm.then_inc(sm["pe_prep"], 1)
        if n == 2:
            wait(pe, "prep_copied", 4)
            for h in range(HEADS):
                mm = pe.matmul(G0[0:16, 0:DIM], avT[:, h], wo[:, h], start=(h == 0), stop=(h == HEADS - 1))
            mm.then_inc(sm["pe_prep"], 1)

    def dve_prep(dve, n):
        if n == 0:
            wait(dve, "weights_in", 16 * N_LOADS)
            wait(dve, "init_done", 11)
            st = Steps(dve, sm["prep_steps"])
            st(dve.tensor_reduce(e4s[:, 0:1], e4[:, :], AX.X, ALU.add))
            st(dve.tensor_scalar(e4s[:, 1:2], e4s[:, 0:1], -1.0 / DIM, None, ALU.mult))
            dve.tensor_scalar(ec[:, :], e4[:, :], e4s[:, 1:2], None, ALU.add).then_inc(sm["prep_copied"], 1)
        if n == 1:
            wait(dve, "pe_prep", 1)
            dve.tensor_copy(ecT[:, :, :], G0[0:KC, 0:8].rearrange("p (c j) -> p c j", c=2)).then_inc(sm["prep_copied"], 1)
            wait(dve, "prep_copied", 2)
            for c in range(2):
                rows = ecT[:, c].unsqueeze(2).to_broadcast([KC, 4, 4])
                cols = ecT[:, c].unsqueeze(1).to_broadcast([KC, 4, 4])
                ins = dve.scalar_tensor_tensor(out=ecP[:, c].rearrange("p (i j) -> p i j", i=4), in0=rows, scalar=1.0 / DIM,
                                               in1=cols, op0=ALU.mult, op1=ALU.mult)
            ins.then_inc(sm["prep_copied"], 1)
        if n == 2:
            wait(dve, "pe_prep", 2)
            dve.tensor_copy(gram[:, :], G1[0:SC, 0:16]).then_inc(sm["mats_ready"], 1)
            dve.tensor_copy(mqk[0:4, :], F[0:4, 0:512]).then_inc(sm["mats_ready"], 1)
            dve.tensor_copy(mout[0:4, DIM:2 * DIM], G0[0:4, 0:DIM]).then_inc(sm["mats_ready"], 1)
            for h in range(HEADS):
                ins = dve.tensor_copy(avT[:, h, 4 * h:4 * h + 4], G1[0:HD, 32 + 4 * h:36 + 4 * h])
            ins.then_inc(sm["prep_copied"], 1)
        if n == 3:
            wait(dve, "pe_prep", 3)
            dve.tensor_copy(mout[64:80, 0:DIM], G0[0:16, 0:DIM]).then_inc(sm["mats_ready"], 1)
            dve.tensor_copy(mout[32:36, 2 * DIM:3 * DIM], e4[:, :]).then_inc(sm["mats_ready"], 1)

    Z_STEPS = 13

    def pool_z(pool, b, par):
        step = Steps(pool, sm["z_steps"], b * Z_STEPS)
        sv = sums[:, par].rearrange("p (c k) -> p c k", c=2)
        z, u = ct[:, par, :, 32:36], ct[:, par, :, 0:4]
        pool.wait_ge(seg["enm_ready"], b + 1)
        wait(pool, "tot_copied", 2 * b + 2)
        step(pool.tensor_tensor(den0[:, :], ntok[:, :], sv[:, :, 4], ALU.subtract))
        step(pool.tensor_tensor(den0[:, :], den0[:, :], enm[:, par:par + 1].to_broadcast([SC, 2]), ALU.mult))
        step(pool.tensor_tensor(den0[:, :], den0[:, :], sv[:, :, 0], ALU.add))
        step(pool.tensor_tensor(den0[:, :], den0[:, :], minus1[:, :], ALU.pow))
        wait(pool, "t2_done", b - 1)
        step(pool.tensor_tensor(z[:, :, 0:3], sv[:, :, 1:4], den0[:, :].unsqueeze(2).to_broadcast([SC, 2, 3]), ALU.mult))
        for c in range(2):
            ins = pool.tensor_tensor(quad[:, c].rearrange("p (i j) -> p i j", i=4), z[:, c].unsqueeze(2).to_broadcast([SC, 4, 4]),
                                     z[:, c].unsqueeze(1).to_broadcast([SC, 4, 4]), ALU.mult)
        step(ins)
        step(pool.tensor_tensor(quad[:, :, :], quad[:, :, :], gram[:, :].unsqueeze(1).to_broadcast([SC, 2, 16]), ALU.mult))
        for m in (8, 4, 2):
            step(pool.tensor_tensor(quad[:, :, 0:m], quad[:, :, 0:m], quad[:, :, m:2 * m], ALU.add))
        step(pool.tensor_tensor(zvar[:, :], quad[:, :, 0], quad[:, :, 1], ALU.add))
        step(pool.tensor_tensor(zvar[:, :], zvar[:, :], eps[:, :], ALU.add))
        step(pool.tensor_tensor(zrstd[:, :], zvar[:, :], mhalf[:, :], ALU.pow))
        pool.tensor_tensor(u, z, zrstd[:, :].unsqueeze(2).to_broadcast([SC, 2, 4]), ALU.mult).then_inc(sm["placed"], 1)

    def pe_t1(pe, b, par):
        wait(pe, "placed", b + 1)
        wait(pe, "xt_ready", b)
        for c in range(2):
            mm = pe.transpose(G0[0:CROWS, SC * c:SC * (c + 1)], ct[:, par, c], ident[0:SC, 0:SC])
        mm.then_inc(sm["t1_done"], 1)

    def act_ct1(act, b):
        wait(act, "t1_done", b + 1)
        act.copy(cT1[:, :], G0[0:CROWS, 0:S]).then_inc(sm["ct1_ready"], 1)

    QK = (G1, G0)

    def pe_qk(pe, b, hp):
        wait(pe, "ct1_ready", b + 1)
        if hp == 0:
            wait(pe, "rd_ready", b)
        for j in range(2):
            mm = pe.matmul(QK[hp][:, j * S:(j + 1) * S], mqk[:, 256 * j + 128 * hp:256 * j + 128 * (hp + 1)], cT1[:, :],
                           start=True, stop=True)
        mm.then_inc(sm["qk_done"], 1)

    def act_elu(act, b, hp):
        wait(act, "qk_done", 2 * b + hp + 1)
        act.activation(expx[:, hp], QK[hp][:, 0:2 * S], ACT.Exp)
        act.activation(relx[:, hp], QK[hp][:, 0:2 * S], ACT.Relu).then_inc(sm["er_ready"], 1)

    def dve_elu(dve, b, hp):
        wait(dve, "er_ready", 2 * b + hp + 1)
        dve.scalar_tensor_tensor(out=qk[:, hp], in0=expx[:, hp], scalar=1.0, in1=relx[:, hp],
                                 op0=ALU.min, op1=ALU.add).then_inc(sm["elu_ready"], 1)

    def pe_scores(pe, b, h):
        hp, r = h // 2, h % 2
        out = QK[r]
        wait(pe, "elu_ready", 2 * b + hp + 1)
        if h == 1:
            wait(pe, "er_ready", 2 * b + 2)
        if h >= 2:
            wait(pe, "at_copied", HEADS * b + h - 1)
        rows = slice(HD * r, HD * (r + 1))
        q, k = qk[rows, hp, 0:S], qk[rows, hp, S:2 * S]
        pe.matmul(out[0:SC, 0:S], k[:, 0:SC], q, start=True, stop=True)
        pe.matmul(out[0:SC, S:S + SC], k[:, SC:S], q[:, SC:S], start=True, stop=True).then_inc(sm["at_done"], 1)

    def act_scores(act, b, h):
        wait(act, "at_done", HEADS * b + h + 1)
        act.copy(aT[:, h], QK[h % 2][0:SC, 0:3 * SC]).then_inc(sm["at_copied"], 1)

    def pool_mask(pool, b, h):
        wait(pool, "at_copied", HEADS * b + h + 1)
        v = aT[:, h].rearrange("p (g i) -> p g i", g=3)[:, 0:3:2]
        pool.tensor_tensor(v, v, tri[0:SC].unsqueeze(1).to_broadcast([SC, 2, SC]), ALU.mult).then_inc(sm["masked"], 1)

    def pe_sums2(pe, b, par):
        wait(pe, "masked", HEADS * (b + 1))
        for h in range(HEADS):
            o = [G1[0:SC, 20 * c + 5 * h:20 * c + 5 * h + 5] for c in range(2)]
            pe.matmul(o[0], aT[:, h, 0:SC], ct[:, par, 0, 0:5], start=True, stop=True)
            pe.matmul(o[1], aT[:, h, SC:2 * SC], ct[:, par, 0, 0:5], start=True, stop=False)
            mm = pe.matmul(o[1], aT[:, h, 2 * SC:3 * SC], ct[:, par, 1, 0:5], start=False, stop=True)
        mm.then_inc(sm["n_done"], 1)

    def dve_y(dve, b, par):
        wait(dve, "n_done", b + 1)
        st = Steps(dve, sm["y_steps"], 2 * b)
        num = G1[0:SC, 0:40].rearrange("p (c h k) -> p c h k", c=2, h=HEADS)
        st(dve.tensor_scalar(den[:, :, :], num[:, :, :, 4], DEN_MIN, None, ALU.max))
        st(dve.reciprocal(rden[:, :, :], den[:, :, :]))
        out = ct[:, par, :, 64:80].rearrange("p c (h k) -> p c h k", h=HEADS)
        dve.tensor_tensor(out, num[:, :, :, 0:4], rden[:, :, :].unsqueeze(3).to_broadcast([SC, 2, HEADS, 4]),
                          ALU.mult).then_inc(sm["y_ready"], 1)

    def pe_t2(pe, b, par):
        wait(pe, "y_ready", b + 1)
        for c in range(2):
            mm = pe.transpose(G0[0:CROWS, SC * c:SC * (c + 1)], ct[:, par, c], ident[0:SC, 0:SC])
        mm.then_inc(sm["t2_done"], 1)

    def act_ct2(act, b):
        wait(act, "t2_done", b + 1)
        act.copy(cT2[:, :], G0[0:CROWS, 0:S]).then_inc(sm["ct2_ready"], 1)

    def pe_out(pe, b, c):
        wait(pe, "ct2_ready", b + 1)
        if c == 0:
            for cc in range(2):
                pe.matmul(G1[0:SC, DIM * cc:DIM * (cc + 1)], cT2[:, SC * cc:SC * (cc + 1)], mout[:, 2 * DIM:3 * DIM],
                          start=True, stop=True)
        else:
            wait(pe, "gated_ready", 2 * b + 1)
        pe.matmul(G0[0:SC, 0:2 * DIM], cT2[:, SC * c:SC * (c + 1)], mout[:, 0:2 * DIM],
                  start=True, stop=True).then_inc(sm["o_done"], 1)

    def act_gate(act, b, c):
        wait(act, "o_done", 2 * b + c + 1)
        act.activation(th[:, c], G0[0:SC, DIM:2 * DIM], ACT.Tanh, scale=0.5).then_inc(sm["th_ready"], 1)

    def dve_h1(dve, b, par, c):
        wait(dve, "th_ready", 2 * b + c + 1)
        dve.scalar_tensor_tensor(out=gated[:, c], in0=th[:, c], scalar=1.0, in1=G0[0:SC, 0:DIM],
                                 op0=ALU.add, op1=ALU.mult).then_inc(sm["gated_ready"], 1)
        wait(dve, "gated_ready", 2 * b + c + 1)
        dve.scalar_tensor_tensor(out=h1[:, par, c], in0=gated[:, c], scalar=0.5, in1=G1[0:SC, DIM * c:DIM * (c + 1)],
                                 op0=ALU.mult, op1=ALU.add).then_inc(sm["h1_ready"], 1)

    def dve_stats2(dve, b, par):
        wait(dve, "h1_ready", 2 * b + 2)
        for c in range(2):
            dve.bn_stats(bns[:, c], h1[:, par, c]).then_inc(sm["var_steps"], 1)
        wait(dve, "var_steps", 2 * b + 2)

    def dve_aggregate(dve, b):
        for c in range(2):
            ins = dve.bn_aggr(mv[:, c], bns[:, c])
        ins.then_inc(sm["var_ready"], 1)

    def pool_rstd(pool, b):
        wait(pool, "var_ready", b + 1)
        pool.tensor_tensor(vare[:, :], mv[:, :, 1], eps[:, :], ALU.add).then_inc(sm["rstd_steps"], 1)
        wait(pool, "rstd_steps", b + 1)
        pool.tensor_tensor(rstd[:, :], vare[:, :], mhalf[:, :], ALU.pow).then_inc(sm["rstd_ready"], 1)

    def dve_x2(dve, b, par):
        wait(dve, "rstd_ready", b + 1)
        for c in range(2):
            ins = dve.tensor_scalar(x2[:, c], h1[:, par, c], mv[:, c, 0:1], rstd[:, c:c + 1], ALU.subtract, ALU.mult)
        ins.then_inc(sm["x2_ready"], 1)

    def pe_t3(pe, b):
        wait(pe, "x2_ready", b + 1)
        for kc in range(2):
            for c in range(2):
                mm = pe.transpose(G0[0:KC, S * kc + SC * c:S * kc + SC * (c + 1)], x2[:, c, KC * kc:KC * (kc + 1)],
                                  ident[0:SC, 0:SC])
        mm.then_inc(sm["t3_done"], 1)

    def act_xt(act, b, par):
        wait(act, "t3_done", b + 1)
        wait(act, "ff_done", 8 * (b - 1))
        act.copy(xT[0:KC, par].rearrange("p k s -> p (k s)"), G0[0:KC, 0:2 * S]).then_inc(sm["xt_ready"], 1)

    def rows_of(t, par, kc, c):
        return t[:, par, kc, SC * c:SC * (c + 1)]

    def pe_router(pe, b, par):
        wait(pe, "xt_ready", b + 1)
        for c in range(2):
            for kc in range(2):
                mm = pe.matmul(G1[0:SC, EXPERTS * c:EXPERTS * (c + 1)], rows_of(xT, par, kc, c), wrt[:, kc],
                               start=(kc == 0), stop=(kc == 1))
        mm.then_inc(sm["r_done"], 1)

    def dve_router1(dve, b):
        wait(dve, "r_done", b + 1)
        dve.tensor_copy(rs[:, :, 0:EXPERTS], G1[0:SC, 0:2 * EXPERTS].rearrange("p (c e) -> p c e", c=2)).then_inc(sm["r_steps"], 1)
        for c in range(2):
            ins = dve.max(rs[:, c, 8:16], G1[0:SC, EXPERTS * c:EXPERTS * (c + 1)])
        ins.then_inc(sm["r_steps"], 1)
        wait(dve, "r_steps", b * N_RSTEPS + 2)
        dve.tensor_tensor(rd[:, :, :], rs[:, :, 0:10], rs[:, :, 8:9].to_broadcast([SC, 2, 10]), ALU.subtract)\
           .then_inc(sm["rd_ready"], 1)

    def act_router(act, b):
        wait(act, "rd_ready", b + 1)
        act.activation(re[:, :, :], rd[:, :, :], ACT.Exp).then_inc(sm["re_ready"], 1)

    N_RSTEPS = 5

    def dve_router2(dve, b, par):
        wait(dve, "re_ready", b + 1)
        st = Steps(dve, sm["r_steps"], b * N_RSTEPS + 2)
        dve.tensor_reduce(rsum[:, :], re[:, :, 0:EXPERTS], AX.X, ALU.add)
        dve.tensor_tensor(rmask[:, :, :], rd[:, :, 0:EXPERTS], rd[:, :, 9:10].to_broadcast([SC, 2, EXPERTS]), ALU.is_ge)
        st(dve.tensor_tensor(rtop[:, :], re[:, :, 8], re[:, :, 9], ALU.add))
        dve.tensor_tensor(rw[:, :, :], rmask[:, :, :], re[:, :, 0:EXPERTS], ALU.mult)
        st(dve.scalar_tensor_tensor(out=rnorm[:, :], in0=rsum[:, :], scalar=TOP_EPS, in1=rtop[:, :], op0=ALU.mult, op1=ALU.add))
        st(dve.reciprocal(rinv[:, :], rnorm[:, :]))
        dve.tensor_tensor(wt[:, par], rw[:, :, :], rinv[:, :].unsqueeze(2).to_broadcast([SC, 2, EXPERTS]), ALU.mult)\
           .then_inc(sm["w_ready"], 1)

    def pe_experts(pe, b, par, n, kc, kept):
        c, pair = n // 4, n % 4
        if kc == 0:
            wait(pe, "mixed", 16 * b + 2 * n)
            if n == 0:
                wait(pe, "tot_copied", 2 * kept)
        mm = pe.matmul(F[0:SC, 0:2 * DIM], rows_of(xT, par, kc, c), wff[:, kc, 2 * DIM * pair:2 * DIM * (pair + 1)],
                       start=(kc == 0), stop=(kc == 1))
        if kc == 1:
            mm.then_inc(sm["ff_done"], 1)

    def dve_mix(dve, b, par, n):
        c, pair = n // 4, n % 4
        wait(dve, "ff_done", 8 * b + n + 1)
        if n == 0:
            wait(dve, "w_ready", b + 1)
            wait(dve, "out_ready", 2 * b - 2)
        for r, mix in ((0, mixa), (1, mixb)):
            e = 2 * pair + r
            y, w = F[0:SC, DIM * r:DIM * (r + 1)], wt[:, par, c, e:e + 1]
            if pair:
                wait(dve, "mixed", 16 * b + 2 * n - 1 + r)
            if pair == 0 and r == 1:
                ins = dve.tensor_scalar(mix[:, par, c], y, w, None, ALU.mult)
            else:
                ins = dve.scalar_tensor_tensor(out=mix[:, par, c], in0=y, scalar=w, in1=(mix if pair else h1)[:, par, c],
                                               op0=ALU.mult, op1=ALU.add)
            ins.then_inc(sm["mixed"], 1)

    def pool_out(pool, b, par, c):
        wait(pool, "mixed", 16 * b + 8 * (c + 1))
        wait(pool, f"stored{par}", 8 * (b - par))
        pool.tensor_tensor(outb[:, par, c], mixa[:, par, c], mixb[:, par, c], ALU.add).then_inc(sm["out_ready"], 1)

    def sp_store(sp, b, par):
        wait(sp, "out_ready", 2 * b + 2)
        sp.dma_start(out_d[b].rearrange("(c p) d -> p c d", c=2), outb[:, par]).then_inc(sm[f"stored{par}"], 16)

    def sp_stored(sp):
        for par in range(2):
            wait(sp, f"stored{par}", 8 * B)

    return dict(sp_weights=sp_weights, sp_store=sp_store, sp_stored=sp_stored, pool_init=pool_init, pool_z=pool_z,
                pool_mask=pool_mask, pool_rstd=pool_rstd, pool_out=pool_out,
                pe_prep=pe_prep, pe_t1=pe_t1, pe_qk=pe_qk, pe_scores=pe_scores, pe_sums2=pe_sums2, pe_t2=pe_t2,
                pe_out=pe_out, pe_t3=pe_t3, pe_router=pe_router, pe_experts=pe_experts,
                act_ct1=act_ct1, act_elu=act_elu, act_scores=act_scores, act_ct2=act_ct2, act_gate=act_gate,
                act_xt=act_xt, act_router=act_router,
                dve_prep=dve_prep, dve_elu=dve_elu, dve_y=dve_y, dve_h1=dve_h1, dve_stats2=dve_stats2,
                dve_aggregate=dve_aggregate, dve_x2=dve_x2, dve_router1=dve_router1, dve_router2=dve_router2,
                dve_mix=dve_mix, mats_ready=sm["mats_ready"], mixed=sm["mixed"])


def build(nc, a, out_d, n_images):
    B = n_images
    with ExitStack() as ctx:
        psum = ctx.enter_context(nc.psum_tensor("psum", [P, 8, 512], F32))[:, :, :]
        pad_d = nc.dram_tensor("planes_pad", [2, PLANES, (H + 2) * PW + 60], BF16).ap()
        g = segment_sums(nc, ctx, a["x"], a["conv_w108"], a["conv_b"], a["score_w"], a["keep"], a["sel"],
                                           pad_d, psum, psum[:, SLOTS + 3])
        t = layer(nc, ctx, B, a, out_d, a["ident"], a["tri"], psum, g)
        block = ctx.enter_context(nc.Block())

        def rounds(eng, one_round):
            def at(r):
                one_round(eng, r // 2, r % 2, r, [0 <= r - j < B for j in range(4)], r + 1 < B, r + 2 < B)

            head = min(6, B)
            for r in range(head):
                at(r)
            if B - 2 > head:
                with eng.Fori(head // 2, B // 2 - 1) as i:
                    for par in range(2):
                        one_round(eng, i, par, None, [True] * 4, True, True)
            for r in range(max(head, B - 2), B + 3):
                at(r)

        def sp_round(sp, i, par, r, does, more, more2):
            if more:
                g["sp_patches"](sp, *image(i, par, 1))
            if more2:
                g["sp_load_x"](sp, i + 1, par)
            if does[3]:
                t["sp_store"](sp, 2 * i + par - 3, 1 - par)

        def pool_round(pool, i, par, r, does, more, more2):
            b = 2 * i + par
            if more:
                g["pool_split"](pool, *image(i, par, 1))
            if r == 1:
                pool.wait_ge(t["mats_ready"], 5)
            if does[1]:
                t["pool_z"](pool, b - 1, 1 - par)
            if does[2]:
                for h in range(HEADS):
                    t["pool_mask"](pool, b - 2, h)
            if more:
                g["pool_features"](pool, *image(i, par, 1))
            if does[3]:
                t["pool_out"](pool, b - 3, 1 - par, 0)
            if does[2]:
                t["pool_rstd"](pool, b - 2)
            if does[3]:
                t["pool_out"](pool, b - 3, 1 - par, 1)

        def pe_round(pe, i, par, r, does, more, more2):
            b = 2 * i + par
            kept = b if r is None else min(r, B)
            if r == 2:
                pe.wait_ge(t["mats_ready"], 5)
            for k in range(NG):
                if does[0]:
                    g["pe_group"](pe, i, par, k, more)
                if r == 0 and k in PE_AT["prep"]:
                    t["pe_prep"](pe, PE_AT["prep"].index(k))
                if does[1] and k == PE_AT["total"]:
                    need(pe, t["mixed"], 16 * (b - 3))
                    g["pe_total"](pe, b - 1, 1 - par)
                if does[2]:
                    if k == PE_AT["t1"]:
                        t["pe_t1"](pe, b - 2, par)
                    if k in PE_AT["qk"]:
                        t["pe_qk"](pe, b - 2, PE_AT["qk"].index(k))
                    if k in PE_AT["scores"]:
                        t["pe_scores"](pe, b - 2, PE_AT["scores"].index(k))
                    if k == PE_AT["sums"]:
                        t["pe_sums2"](pe, b - 2, par)
                    if k == PE_AT["t2"]:
                        t["pe_t2"](pe, b - 2, par)
                    if k in PE_AT["out"]:
                        t["pe_out"](pe, b - 2, PE_AT["out"].index(k))
                    if k == PE_AT["t3"]:
                        t["pe_t3"](pe, b - 2)
                    if k == PE_AT["router"]:
                        t["pe_router"](pe, b - 2, par)
                if does[3] and k in PE_AT["experts"]:
                    half = PE_AT["experts"].index(k)
                    t["pe_experts"](pe, b - 3, 1 - par, half // 2, half % 2, kept)

        def act_round(act, i, par, r, does, more, more2):
            b = 2 * i + par
            for k in range(NG):
                if does[0]:
                    g["act_group"](act, b, k)
                if more and k == ACT_AT["e"]:
                    g["act_e"](act, b + 1, 1 - par)
                if does[2]:
                    if k == ACT_AT["ct1"]:
                        t["act_ct1"](act, b - 2)
                    if k in ACT_AT["elu"]:
                        t["act_elu"](act, b - 2, ACT_AT["elu"].index(k))
                    if k in ACT_AT["scores"]:
                        t["act_scores"](act, b - 2, ACT_AT["scores"].index(k))
                    if k == ACT_AT["ct2"]:
                        t["act_ct2"](act, b - 2)
                    if k in ACT_AT["gate"]:
                        t["act_gate"](act, b - 2, ACT_AT["gate"].index(k))
                    if k == ACT_AT["xt"]:
                        t["act_xt"](act, b - 2, par)
                if does[3] and k == ACT_AT["router"]:
                    t["act_router"](act, b - 3)

        def dve_round(dve, i, par, r, does, more, more2):
            b = 2 * i + par
            for k in range(NG):
                if does[0]:
                    g["dve_group"](dve, b, k)
                if r == 0 and k in DVE_AT["prep"]:
                    t["dve_prep"](dve, DVE_AT["prep"].index(k))
                if does[1] and k == DVE_AT["copy"]:
                    g["dve_copy_acc"](dve, b - 1, 1 - par)
                if does[1] and k == DVE_AT["keep"]:
                    g["dve_keep"](dve, b - 1, 1 - par)
                if more and k == DVE_AT["pmax"]:
                    g["dve_pmax"](dve, b + 1, 1 - par)
                if more and k == DVE_AT["negm"]:
                    g["dve_negm"](dve, b + 1, 1 - par)
                if does[3] and k == DVE_AT["router1"]:
                    t["dve_router1"](dve, b - 3)
                if does[3] and k == DVE_AT["router2"]:
                    t["dve_router2"](dve, b - 3, 1 - par)
                if does[3] and k in DVE_AT["mix"]:
                    t["dve_mix"](dve, b - 3, 1 - par, DVE_AT["mix"].index(k))
                if does[2]:
                    if k in DVE_AT["elu"]:
                        t["dve_elu"](dve, b - 2, DVE_AT["elu"].index(k))
                    if k == DVE_AT["y"]:
                        t["dve_y"](dve, b - 2, par)
                    if k in DVE_AT["h1"]:
                        t["dve_h1"](dve, b - 2, par, DVE_AT["h1"].index(k))
                    if k == DVE_AT["h1"][1]:
                        t["dve_stats2"](dve, b - 2, par)
                    if k == DVE_AT["aggregate"]:
                        t["dve_aggregate"](dve, b - 2)
                    if k == DVE_AT["x2"]:
                        t["dve_x2"](dve, b - 2, par)

        @block.sync
        def _(sp):
            g["sp_constants"](sp)
            g["sp_start"](sp)
            t["sp_weights"](sp)
            rounds(sp, sp_round)
            t["sp_stored"](sp)

        @block.gpsimd
        def _(pool):
            g["pool_init"](pool)
            g["pool_split"](pool, 0, 0)
            t["pool_init"](pool)
            g["pool_features"](pool, 0, 0)
            rounds(pool, pool_round)

        @block.tensor
        def _(pe):
            g["pe_start"](pe)
            rounds(pe, pe_round)

        @block.scalar
        def _(act):
            act.preload_act_table(ACT.Exp)
            g["act_e"](act, 0, 0)
            rounds(act, act_round)

        @block.vector
        def _(dve):
            g["dve_start"](dve)
            rounds(dve, dve_round)


def kernel(**inputs):
    import numpy as _np
    import concourse.bacc as _bacc
    from concourse import mybir as _mybir
    from concourse.bass_utils import run_bass_kernel_spmd as _run

    given = {k: _np.asarray(v) for k, v in inputs.items()}
    arrays = layout(given)
    n_images = given["x"].shape[0]
    nc = _bacc.Bacc("TRN2", target_bir_lowering=False, num_devices=1)
    aps = {n: nc.dram_tensor(f"in_{n}", v.shape, _mybir.dt.from_np(v.dtype), kind="ExternalInput").ap()
           for n, v in arrays.items()}
    out_d = nc.dram_tensor("out", (n_images, S, DIM), _mybir.dt.float32, kind="ExternalOutput").ap()
    build(nc, aps, out_d, n_images)
    r = _run(nc, [{f"in_{n}": v for n, v in arrays.items()}], core_ids=[0])
    return r.results[0]["out"]


def layout(given):
    keep, sel, ident, tri = constants()
    w = given["L0_tok_conv_w"].transpose(2, 3, 1, 0).reshape(TAPS, 1, C, S)
    arrays = {
        "x": given["x"],
        "conv_w108": np.broadcast_to(w, (TAPS, PLANES // C, C, S)).reshape(TAPS * PLANES, S),
        "conv_b": given["L0_tok_conv_b"],
        "score_w": given["L0_tok_score_w"],
        "embed_w": given["L0_tok_embed_w"],
        "embed_b": given["L0_tok_embed_b"],
        "Wq": given["L0_attn_Wq"], "Wk": given["L0_attn_Wk"], "Wv": given["L0_attn_Wv"],
        "Wo": given["L0_attn_Wo"], "Wg": given["L0_attn_Wg"],
        "router_wT": given["L0_ffn_router_w"].T,
        "router_b": given["L0_ffn_router_b"],
        "expert_wT": given["L0_ffn_expert_w"].transpose(0, 2, 1),
        "expert_b": given["L0_ffn_expert_b"],
        "keep": keep, "sel": sel, "ident": ident, "tri": tri,
    }
    return {n: np.ascontiguousarray(v) for n, v in arrays.items()}
```

```python
from contextlib import ExitStack

import numpy as np
import concourse.bass as bass
from concourse import mybir

ALU = mybir.AluOpType
ACT = mybir.ActivationFunctionType
AX = mybir.AxisListType
RED = bass.bass_isa.ReduceOp
F32 = mybir.dt.float32
BF16 = mybir.dt.bfloat16

P = 128
H = W = 128
C = 3
S = 196
SC = S // 2
PW = W + 2
TAPS = 9
PLANES = 12
KROWS = TAPS * PLANES + 2
LOGIT_SCALE = 2.0 ** 64
ONES_PAIR = float(np.array([0x3F803F80], np.uint32).view(np.float32)[0])
NF = 13
NSUM = 5
ROWS = 64
HALF = 32
ONE_ROW = 24
CROWS = P

GROUPS = [2] * (W // 2 - 1) + [1, 1]
STARTS = [sum(GROUPS[:k]) for k in range(len(GROUPS))]
NG = len(GROUPS)
SLOTS = 5
RING = 13
assert NG % SLOTS == 0 and NG % RING == 0

BY_DVE = (5, 12, 30, 42, 47, 49, 50)
PE_AT = dict(t2=0, t3=2, total=1, t1=7, router=8, qk=(12, 16), out=(22, 29), h=31, scores=(34, 39, 42, 45), sums=(53,
             54, 55, 56), experts=(11, 12, 13, 14, 18, 19, 20, 21, 24, 25, 26, 27, 31, 32, 33, 34, 38, 39, 40, 41, 44,
             45, 46, 47, 51, 52, 53, 54, 56, 57, 58, 59), prep=(12, 22, 34))
ACT_AT = dict(ct2=2, xt=5, ct1=11, router=13, elu=(14, 19), gate=(25, 31), e=29, scores=(38, 41, 45, 49))
DVE_AT = dict(copy=3, keep=9, router1=13, router2=17, pmax=19, elu=(18, 24), negm=28, gated=(29, 34), h1=36,
              aggregate=42, y=61, mix=(18, 19, 25, 26, 33, 34, 39, 40, 46, 47, 51, 52, 57, 58, 63, 64), prep=(8, 16,
              28, 40))


def constants():
    keep = np.ones((KROWS, 2), np.float32)
    q3 = np.array([(r % PLANES) >= 9 for r in range(TAPS * PLANES)] + [False, True])
    keep[:, 0] = ~q3
    keep[:, 1] = q3
    sel = np.zeros((P, NSUM), np.float32)
    for r in range(P):
        if r % 32 < 12:
            sel[r, (r % 32) % 4] = 1.0
        elif r % 32 == 12:
            sel[r, 4] = 1.0
    tri = np.triu(np.ones((SC, SC), np.float32))
    place = np.zeros((5, ROWS), np.float32)
    parts = np.zeros((ROWS, 3), np.float32)
    for g, part in enumerate((0, 1, 2, 0, 1, 0)):
        for j in range(4):
            place[j, HALF + 4 * g + j] = 1.0
            parts[[4 * g + j, HALF + 4 * g + j], part] = 1.0
    place[4, ONE_ROW] = 1.0
    parts[ONE_ROW, 0] = 1.0
    return keep, sel, np.eye(P, dtype=np.float32), tri, place, parts


class Steps:

    def __init__(self, eng, sem, base=0):
        self.eng, self.sem, self.value = eng, sem, base

    def __call__(self, ins):
        ins.then_inc(self.sem, 1)
        self.value = self.value + 1
        self.eng.wait_ge(self.sem, self.value)


def need(eng, sem, value):
    if isinstance(value, int) and value <= 0:
        return
    eng.wait_ge(sem, value)


def image(i, par, shift):
    return i + (par + shift) // 2, (par + shift) % 2


def by_dve(k):
    return k in BY_DVE


def made(k):
    return by_dve(k), sum(1 for j in range(k + 1) if by_dve(j) == by_dve(k))


N_DVE = sum(1 for k in range(NG) if by_dve(k))
N_ACT = NG - N_DVE
assert not by_dve(NG - 1)


def segment_sums(nc, ctx, x, conv_w108, conv_b, score_w, keep_d, sel_d, pad_d, psum, tot):
    B = x.shape[0]
    x_v = x.rearrange("b c h w -> b h c w")

    def sb(name, shape, dt):
        return ctx.enter_context(nc.sbuf_tensor(name, shape, dt))

    def sem(name):
        return ctx.enter_context(nc.semaphore(name))

    patches = sb("patches", [P, 2, H * PW], BF16)
    xin = sb("xin", [P, 2, C, W], F32)
    xs = sb("xs", [P, 2, 9, PW], BF16)
    xres = sb("xres", [P, C, W], F32)
    score = sb("score", [P, 2, W], F32)
    term = sb("term", [P, C, W], F32)
    feat = sb("feat", [P, 2, 4, W], F32)
    fres = sb("fres", [P, 4, W], F32)
    fs = sb("fs", [P, 2, 32, W], BF16)
    pmax = sb("pmax", [P, 2], F32)
    imax = sb("imax", [P, 2], F32)
    negm = sb("negm", [P, 2], F32)
    onehot = sb("onehot", [P, RING, 2, S], BF16)
    negmx = sb("negmx", [P, RING, 2], F32)
    scw = sb("scw", [P, C], F32)
    wrep = sb("wrep", [P, S], F32)
    wsc = sb("wsc", [P, S], F32)
    wres = sb("wres", [P, S], F32)
    w1 = sb("w1", [P, S], BF16)
    w2 = sb("w2", [P, S], BF16)
    w3 = sb("w3", [P, S], BF16)
    w3k = sb("w3k", [P, S], BF16)
    wA = sb("wA", [P, S], BF16)
    wB = sb("wB", [P, S], BF16)
    keep = sb("keep", [P, 2], F32)
    sel = sb("sel", [P, NSUM], F32)
    accs = sb("accs", [P, 2, S], F32)
    zero = sb("zero", [P, 1], F32)
    zrow = sb("zrow", [PLANES, PW], BF16)
    logits = [psum[:, s] for s in range(SLOTS)]
    acc = psum[:, SLOTS]
    enm = sb("enm", [SC, 2], F32)
    ct = sb("ct", [SC, 2, 2, CROWS], F32)
    zu = sb("zu", [SC, 2, 4, 4], F32)
    sums = sb("sums", [SC, 2, 2 * NSUM], F32)

    consts_in = sem("consts_in")
    borders_out = sem("borders_out")
    pool_init_done = sem("pool_init")
    ones_even = sem("ones_even")
    ones_odd = sem("ones_odd")
    conv_w_ready = sem("conv_w_ready")
    dve_steps = sem("dve_steps")
    x_in = [sem(f"x_in{p}") for p in range(2)]
    split_done = sem("split_done")
    planes_out = [sem(f"planes_out{p}") for p in range(2)]
    patches_in = [sem(f"patches_in{p}") for p in range(2)]
    pool_steps = sem("pool_steps")
    score_ready = sem("score_ready")
    pmax_ready = sem("pmax_ready")
    imax_ready = sem("imax_ready")
    negm_ready = sem("negm_ready")
    enm_ready = sem("enm_ready")
    placed = sem("placed")
    t2_done = sem("t2_done")
    e_ready = sem("e_ready")
    feats_ready = sem("feats_ready")
    logits_ready = sem("logits_ready")
    max_ready = sem("max_ready")
    hot_act = sem("hot_act")
    hot_dve = sem("hot_dve")
    image_done = sem("image_done")
    acc_copied = sem("acc_copied")
    tot_ready = sem("tot_ready")
    tot_copied = sem("tot_copied")

    x_v = x.rearrange("b c h w -> b h c w")

    pad_v = [pad_d[p, :, 0:(H + 2) * PW].rearrange("q (h w) -> h q w", w=PW)[1:H + 1] for p in range(2)]

    def sp_load_x(sp, n, par):
        need(sp, feats_ready, 2 * n + par - 1)
        sp.dma_start(xin[:, par], x_v[2 * n + par]).then_inc(x_in[par], 16)

    def sp_patches(sp, n, par):
        sp.wait_ge(split_done, 2 * n + par + 1)
        sp.dma_start(pad_v[par][:, 0:9, :], xs[:, par]).then_inc(planes_out[par], 16)
        sp.dma_start(pad_v[par][:, 9:12, :], xs[:, par, 0:3]).then_inc(planes_out[par], 16)
        sp.wait_ge(planes_out[par], n * 32 + 32)
        need(sp, image_done, 2 * n + par - 1)
        for j in range(TAPS):
            off = (j // 3) * PW + j % 3
            sp.dma_start(patches[j * PLANES:(j + 1) * PLANES, par], pad_d[par, :, off:off + H * PW]).then_inc(patches_in[par], 16)

    def sp_constants(sp):
        sp.dma_start(wrep[0:KROWS - 2], conv_w108).then_inc(consts_in, 16)
        for r in (KROWS - 2, KROWS - 1):
            sp.dma_start(wrep[r:r + 1], conv_b.rearrange("(a s) -> a s", a=1)).then_inc(consts_in, 16)
        sp.dma_start(keep[0:KROWS], keep_d).then_inc(consts_in, 16)
        sp.dma_start(sel[:, :], sel_d).then_inc(consts_in, 16)
        sp.dma_start(scw[:, :], score_w.rearrange("(a c) -> a c", a=1).to_broadcast([P, C])).then_inc(consts_in, 16)
        sp_load_x(sp, 0, 0)
        sp_load_x(sp, 0, 1)

    def sp_start(sp):
        sp.wait_ge(pool_init_done, 1)
        for p in range(2):
            for r in (0, H + 1):
                sp.dma_start(pad_d[p, :, r * PW:(r + 1) * PW], zrow[:, :]).then_inc(borders_out, 16)
            tail = pad_d.shape[2] - (H + 2) * PW
            sp.dma_start(pad_d[p, :, (H + 2) * PW:], zrow[:, 0:tail]).then_inc(borders_out, 16)
        sp.wait_ge(borders_out, 96)
        sp.wait_ge(ones_even, 1)
        sp_patches(sp, 0, 0)

    POOL_STEPS = 9

    def zeros(m):
        return zero[:, 0:1].unsqueeze(2).to_broadcast([P, m, W])

    def pool_split(pool, n, par):
        b = 2 * n + par
        step = Steps(pool, pool_steps, b * POOL_STEPS)
        X = xin[:, par]
        x1, x2, x3 = (xs[:, par, 3 * q:3 * q + 3, 1:W + 1] for q in range(3))
        pool.wait_ge(x_in[par], n * 16 + 16)
        need(pool, e_ready, b - 1)
        step(pool.tensor_tensor(term[:, :, :], X, scw[:, :].unsqueeze(2).to_broadcast([P, C, W]), ALU.mult))
        step(pool.tensor_tensor(term[:, 0], term[:, 0], term[:, 1], ALU.add))
        pool.tensor_tensor(score[:, par], term[:, 0], term[:, 2], ALU.add).then_inc(score_ready, 1)
        need(pool, patches_in[par], n * (16 * TAPS))
        step(pool.tensor_tensor(x1, X, zeros(C), ALU.add))
        step(pool.tensor_tensor(xres[:, :, :], X, x1, ALU.subtract))
        step(pool.tensor_tensor(x2, xres[:, :, :], zeros(C), ALU.add))
        pool.wait_ge(pmax_ready, b + 1)
        pool.tensor_tensor(x3, xres[:, :, :], x2, ALU.subtract).then_inc(split_done, 1)
        pool.partition_all_reduce(imax[:, par:par + 1], pmax[:, par:par + 1], P, RED.max).then_inc(imax_ready, 1)

    def pool_features(pool, n, par):
        b = 2 * n + par
        step = Steps(pool, pool_steps, b * POOL_STEPS + 5)
        X = xin[:, par]
        f1, f2, f3 = (fs[:, par, 4 * q:4 * q + 4] for q in range(3))
        pool.wait_ge(split_done, b + 1)
        pool.wait_ge(e_ready, b + 1)
        step(pool.tensor_tensor(feat[:, par, 1:4], X, feat[:, par, 0:1].to_broadcast([P, C, W]), ALU.mult))
        need(pool, image_done, b - 1)
        step(pool.tensor_tensor(f1, feat[:, par], zeros(4), ALU.add))
        step(pool.tensor_tensor(fres[:, :, :], feat[:, par], f1, ALU.subtract))
        step(pool.tensor_tensor(f2, fres[:, :, :], zeros(4), ALU.add))
        pool.tensor_tensor(f3, fres[:, :, :], f2, ALU.subtract).then_inc(feats_ready, 1)
        pool.wait_ge(feats_ready, b + 1)

    def pool_init(pool):
        pool.memset(zrow[:, :], 0.0).then_inc(pool_init_done, 1)
        pool.memset(zero[:, :], 0.0).then_inc(pool_init_done, 1)
        for p in range(2):
            pool.memset(xs[:, p], 0.0).then_inc(pool_init_done, 1)
            pool.memset(fs[:, p, 12:13], 1.0).then_inc(pool_init_done, 1)
            pool.memset(fs[:, p, 13:32], 0.0).then_inc(pool_init_done, 1)
        pool.wait_ge(pool_init_done, 8)
        pool.wait_ge(consts_in, 96)

    def pool_ones(pool):
        pool.wait_ge(imax_ready, 1)
        pool.memset(patches[96:P, 1].bitcast(F32), ONES_PAIR).then_inc(ones_odd, 1)
        pool.wait_ge(ones_odd, 1)

    LAG = SLOTS
    FIRST_SUMS = 2
    tap_rows = [patches[:, p].rearrange("q (h w) -> q h w", w=PW) for p in range(2)]

    def wait_hot(pe, b, k):
        dve_made, count = made(k)
        if dve_made:
            need(pe, hot_dve, b * N_DVE + count)
        else:
            need(pe, hot_act, b * N_ACT + count)

    def pe_logits(pe, b, par, k):
        if k >= SLOTS:
            wait_hot(pe, b, k - SLOTS)
        else:
            wait_hot(pe, b - 1, k - SLOTS + NG)
        for t in range(GROUPS[k]):
            w = STARTS[k] + t
            out = logits[k % SLOTS][:, t * S:(t + 1) * S]
            pe.matmul(out, tap_rows[par][:, :, w], wA[:, :], start=True, stop=False, skip_group_check=True)
            mm = pe.matmul(out, tap_rows[par][:, :, w], wB[:, :], start=False, stop=True, skip_group_check=True)
        mm.then_inc(logits_ready, 1)

    def pe_sums(pe, b, par, k):
        if k == 0:
            pe.wait_ge(feats_ready, b + 1)
            need(pe, acc_copied, b)
        wait_hot(pe, b, k)
        for t in range(GROUPS[k]):
            w = STARTS[k] + t
            q = w % 4
            mm = pe.matmul(acc[32 * q:32 * q + 32, 0:S], fs[:, par, :, w], onehot[:, k % RING, t],
                           start=(w < 4), stop=(w >= W - 4), skip_group_check=True)
        if k == NG - 1:
            mm.then_inc(image_done, 1)

    def pe_total(pe, b, par):
        pe.wait_ge(acc_copied, b + 1)
        for c in range(2):
            mm = pe.matmul(tot[0:SC, NSUM * c:NSUM * (c + 1)], accs[:, par, SC * c:SC * (c + 1)], sel[:, :],
                           start=True, stop=True)
        mm.then_inc(tot_ready, 1)

    def pe_group(pe, i, par, k, more):
        b = 2 * i + par
        if k + LAG < NG:
            pe_logits(pe, b, par, k + LAG)
        elif more:
            n1, par1 = image(i, par, 1)
            if k + LAG == NG:
                pe.wait_ge(patches_in[par1], n1 * (16 * TAPS) + 16 * TAPS)
            pe_logits(pe, b + 1, par1, k + LAG - NG)
        if k >= FIRST_SUMS:
            for j in range(0 if k == FIRST_SUMS else k, k + 1):
                pe_sums(pe, b, par, j)

    def pe_start(pe):
        pe.wait_ge(conv_w_ready, 1)
        pe.wait_ge(patches_in[0], 16 * TAPS)
        for k in range(LAG):
            pe_logits(pe, 0, 0, k)

    def dve_pmax(dve, b, par):
        dve.wait_ge(score_ready, b + 1)
        dve.tensor_reduce(pmax[:, par:par + 1], score[:, par], AX.X, ALU.max).then_inc(pmax_ready, 1)

    def dve_negm(dve, b, par):
        dve.wait_ge(imax_ready, b + 1)
        need(dve, enm_ready, b - 1)
        dve.tensor_scalar(negm[:, par:par + 1], imax[:, par:par + 1], -1.0, 0.0, ALU.mult, ALU.min).then_inc(negm_ready, 1)

    def dve_copy_acc(dve, b, par):
        dve.wait_ge(image_done, b + 1)
        dve.tensor_copy(accs[:, par], acc[:, 0:S]).then_inc(acc_copied, 1)

    def dve_keep(dve, b, par):
        dve.wait_ge(tot_ready, b + 1)
        need(dve, placed, b - 1)
        dve.tensor_copy(sums[:, par], tot[0:SC, 0:2 * NSUM]).then_inc(tot_copied, 1)
        dve.tensor_scalar(zu[:, par, 1:4:2, 3], tot[0:SC, 0:2 * NSUM].rearrange("p (c k) -> p c k", c=2)[:, :, 4], 0.0, None,
                          ALU.is_gt).then_inc(tot_copied, 1)

    def dve_group(dve, b, k):
        dve.wait_ge(logits_ready, b * NG + k + 1)
        m = GROUPS[k]
        src = logits[k % SLOTS][:, 0:m * S].rearrange("p (t s) -> p t s", t=m)
        dve.tensor_reduce(negmx[:, k % RING, 0:m], src, AX.X, ALU.max, negate=True).then_inc(max_ready, 1)
        if k and by_dve(k - 1):
            dve.wait_ge(max_ready, b * NG + k)
            m = GROUPS[k - 1]
            dve.scalar_tensor_tensor(
                out=onehot[:, (k - 1) % RING, 0:m], in0=logits[(k - 1) % SLOTS][:, 0:m * S].rearrange("p (t s) -> p t s", t=m),
                scalar=-1.0, in1=negmx[:, (k - 1) % RING, 0:m].unsqueeze(2).to_broadcast([P, m, S]),
                op0=ALU.mult, op1=ALU.is_equal).then_inc(hot_dve, 1)

    def dve_start(dve):
        steps = [0]

        def step(ins):
            ins.then_inc(dve_steps, 1)
            steps[0] += 1
            dve.wait_ge(dve_steps, steps[0])

        dve.memset(patches[96:P, 0].bitcast(F32), ONES_PAIR).then_inc(ones_even, 1)
        step(dve.memset(wA[96:P], 0.0))
        step(dve.memset(wB[96:P], 0.0))
        K = KROWS
        dve.wait_ge(consts_in, 96)
        step(dve.tensor_scalar(wsc[0:K], wrep[0:K], LOGIT_SCALE, None, ALU.mult))
        step(dve.tensor_copy(w1[0:K], wsc[0:K]))
        step(dve.tensor_tensor(wres[0:K], wsc[0:K], w1[0:K], ALU.subtract))
        step(dve.tensor_copy(w2[0:K], wres[0:K]))
        step(dve.tensor_tensor(w3[0:K], wres[0:K], w2[0:K], ALU.subtract))
        step(dve.tensor_scalar(w3k[0:K], w3[0:K], keep[0:K, 1:2], None, ALU.mult))
        step(dve.scalar_tensor_tensor(out=wA[0:K], in0=w1[0:K], scalar=keep[0:K, 0:1], in1=w3k[0:K], op0=ALU.mult, op1=ALU.add))
        dve.tensor_scalar(wB[0:K], w2[0:K], keep[0:K, 0:1], None, ALU.mult).then_inc(conv_w_ready, 1)
        dve_pmax(dve, 0, 0)
        dve_negm(dve, 0, 0)

    def act_e(act, b, par):
        act.wait_ge(negm_ready, b + 1)
        need(act, placed, b - 1)
        act.activation(feat[:, par, 0], score[:, par], ACT.Exp, bias=negm[:, par:par + 1]).then_inc(e_ready, 1)
        act.activation(enm[:, par:par + 1], negm[0:SC, par:par + 1], ACT.Exp).then_inc(enm_ready, 1)

    def act_group(act, b, k):
        if by_dve(k):
            return
        act.wait_ge(max_ready, b * NG + k + 1)
        for t in range(GROUPS[k]):
            hot = act.activation(onehot[:, k % RING, t], logits[k % SLOTS][:, t * S:(t + 1) * S],
                                 ACT.Exp, bias=negmx[:, k % RING, t:t + 1])
        hot.then_inc(hot_act, 1)

    return dict(sp_constants=sp_constants, sp_start=sp_start, sp_load_x=sp_load_x, sp_patches=sp_patches,
                ones_odd=ones_odd, pool_init=pool_init, pool_ones=pool_ones, pool_split=pool_split, pool_features=pool_features,
                pe_start=pe_start, pe_group=pe_group, pe_total=pe_total,
                dve_start=dve_start, dve_pmax=dve_pmax, dve_negm=dve_negm, dve_copy_acc=dve_copy_acc, dve_keep=dve_keep,
                dve_group=dve_group, act_e=act_e, act_group=act_group,
                enm=enm, sums=sums, tot_copied=tot_copied, enm_ready=enm_ready, placed=placed,
                t2_done=t2_done, ct=ct, zu=zu)


DIM = 192
HEADS, HD = 4, 64
EXPERTS = 8
MALL = 2 * HEADS * HD + 2 * DIM
KC = DIM // 2
NTOK = H * W
LN_EPS = 1e-5
DEN_MIN = 1e-6
TOP_EPS = 1e-9


def layer(nc, ctx, B, wd, out_d, identity_d, tri_d, psum, seg):
    def sb(name, shape, dt=F32):
        return ctx.enter_context(nc.sbuf_tensor(name, shape, dt))

    def sem(name):
        return ctx.enter_context(nc.semaphore(name))

    ident = sb("ident", [P, P])
    tri = sb("tri", [P, SC])
    e4 = sb("e4", [4, DIM])
    e4s = sb("e4s", [4, 2])
    ec = sb("ec", [4, DIM])
    ecT = sb("ecT", [KC, 2, 4])
    ecP = sb("ecP", [KC, 2, 16])
    ones = sb("ones", [P, SC])
    gram = sb("gram", [SC, 16])
    wqk = sb("wqk", [KC, 2, 2 * HEADS * HD])
    wg = sb("wg", [KC, 2, DIM])
    wv = sb("wv", [KC, 2, HEADS * HD])
    wo = sb("wo", [HD, HEADS, DIM])
    avT = sb("avT", [HD, HEADS, 16])
    mo = sb("mo", [CROWS, DIM])
    ecR = sb("ecR", [KC, 2, ROWS])
    place = sb("place", [4, ROWS])
    place1 = sb("place1", [1, ROWS])
    parts = sb("parts", [ROWS, 3])
    onerow = sb("onerow", [1, 2 * HEADS * HD])
    zero1 = sb("zero1", [SC, 1])
    mall = sb("mall", [ROWS, MALL])
    m1 = sb("m1", [ROWS, MALL], BF16)
    m2 = sb("m2", [ROWS, MALL], BF16)
    mb = sb("mb", [ROWS, MALL], BF16)
    wrt = sb("wrt", [P, 2, EXPERTS])
    wff = sb("wff", [P, 2, EXPERTS * DIM])

    den0 = sb("den0", [SC, 2])
    quad = sb("quad", [SC, 2, 16])
    zvar = sb("zvar", [SC, 2])
    zrstd = sb("zrstd", [SC, 2])
    ntok = sb("ntok", [SC, 2])
    minus1 = sb("minus1", [P, 2])
    mhalf = sb("mhalf", [SC, 2])
    eps = sb("eps", [SC, 2])
    ct, zu = seg["ct"], seg["zu"]
    ctb = sb("ctb", [SC, 2, 2, ROWS], BF16)
    zres = sb("zres", [SC, 4, 4])
    identb = sb("identb", [P, P], BF16)
    cTb = sb("cTb", [ROWS, 2, S], BF16)
    cT2 = sb("cT2", [CROWS, S])
    expx = sb("expx", [P, 2, 2 * S])
    qk = sb("qk", [P, 2, 2 * S])
    aT = sb("aT", [SC, HEADS, 3 * SC])
    den = sb("den", [SC, 2, HEADS])
    rden = sb("rden", [SC, 2, HEADS])
    th = sb("th", [SC, 2, DIM])
    gated = sb("gated", [SC, 2, DIM])
    h1 = sb("h1", [SC, 2, 2, DIM])
    bns = sb("bns", [SC, 2, 6])
    mv = sb("mv", [SC, 2, 2])
    vare = sb("vare", [SC, 2])
    rstd = sb("rstd", [SC, 2])
    x2 = sb("x2", [SC, 2, DIM])
    xT = sb("xT", [P, 2, 2, S])
    rs = sb("rs", [SC, 2, 16])
    rd = sb("rd", [SC, 2, 10])
    re = sb("re", [SC, 2, 10])
    rsum = sb("rsum", [SC, 2])
    rtop = sb("rtop", [SC, 2])
    rnorm = sb("rnorm", [SC, 2])
    rinv = sb("rinv", [SC, 2])
    rmask = sb("rmask", [SC, 2, EXPERTS])
    rw = sb("rw", [SC, 2, EXPERTS])
    wt = sb("wt", [SC, 2, 2, EXPERTS])
    mixa = sb("mixa", [SC, 2, 2, DIM])
    mixb = sb("mixb", [SC, 2, 2, DIM])
    outb = sb("outb", [SC, 2, 2, DIM])

    names = ("weights_in init_done pads_done pe_prep prep_copied prep_steps mats_ready z_steps "
             "t1_done ct1_ready qk_done er_ready elu_ready at_done at_copied masked n_done y_steps y_ready "
             "ct2_ready h_done o_done th_ready gated_ready h1_ready var_steps var_ready rstd_steps rstd_ready x2_steps x2_ready t3_done xt_ready "
             "r_done r_steps rd_ready re_ready w_ready ff_done mixed out_ready stored0 stored1").split()
    sm = {n: sem(n) for n in names}
    for n in ("placed", "tot_copied", "t2_done"):
        sm[n] = seg[n]
    enm, sums = seg["enm"], seg["sums"]

    def wait(eng, name, value):
        if isinstance(value, int) and value <= 0:
            return
        eng.wait_ge(sm[name], value)

    G, F = psum[:, SLOTS + 1], psum[:, SLOTS + 2]

    def sp_weights(sp):
        n = [0]

        def load(dst, src):
            sp.dma_start(dst, src).then_inc(sm["weights_in"], 16)
            n[0] += 1

        load(ident[:, :], identity_d)
        load(tri[0:SC, :], tri_d)
        load(place[:, :], wd["place"][0:4])
        load(place1[:, :], wd["place"][4:5])
        load(parts[:, :], wd["parts"])
        load(e4[0:3, :], wd["embed_w"])
        load(e4[3:4, :], wd["embed_b"].rearrange("(a d) -> a d", a=1))
        for j, m in enumerate(("Wq", "Wk")):
            load(wqk[:, :, j * 256:(j + 1) * 256], wd[m].rearrange("(c p) n -> p c n", p=KC))
        load(wg[:, :, :], wd["Wg"].rearrange("(c p) n -> p c n", p=KC))
        load(wv[:, :, :], wd["Wv"].rearrange("(c p) n -> p c n", p=KC))
        load(wo[:, :, :], wd["Wo"].rearrange("(h p) n -> p h n", p=HD))
        load(wrt[0:KC], wd["router_wT"].rearrange("(c p) e -> p c e", p=KC))
        wait(sp, "pads_done", 2)
        load(wrt[KC:KC + 1, 0, :], wd["router_b"].rearrange("(a d) -> a d", a=1))
        for c in range(2):
            load(wff[0:KC, c].rearrange("p (e d) -> p e d", e=EXPERTS), wd["expert_wT"][:, c * KC:(c + 1) * KC, :].rearrange("e p d -> p e d"))
        load(wff[KC:KC + 1, 0, :], wd["expert_b"].rearrange("e d -> (e d)").rearrange("(a n) -> a n", a=1))
        assert n[0] == N_LOADS, n

    N_LOADS = 17

    def pool_init(pool):
        for t, value in ((ct[:, :, :, :], 0.0), (mo[:, :], 0.0), (onerow[:, :], 1.0), (avT[:, :, :], 0.0)):
            pool.memset(t, value).then_inc(sm["init_done"], 1)
        wait(pool, "init_done", 4)
        pool.memset(wrt[KC:P], 0.0).then_inc(sm["pads_done"], 1)
        pool.memset(wff[KC:P], 0.0).then_inc(sm["pads_done"], 1)
        wait(pool, "pads_done", 2)
        pool.memset(ones[:, :], 1.0).then_inc(sm["init_done"], 1)
        pool.memset(mhalf[:, :], -0.5).then_inc(sm["init_done"], 1)
        wait(pool, "init_done", 6)
        pool.memset(eps[:, :], LN_EPS).then_inc(sm["init_done"], 1)
        wait(pool, "init_done", 7)
        pool.memset(xT[KC:P], 1.0).then_inc(sm["init_done"], 1)
        wait(pool, "init_done", 8)
        pool.memset(ct[:, :, :, 4:5], 1.0).then_inc(sm["init_done"], 1)
        wait(pool, "init_done", 9)
        pool.memset(ntok[:, :], float(NTOK)).then_inc(sm["init_done"], 1)
        pool.memset(minus1[:, :], -1.0).then_inc(sm["init_done"], 1)
        wait(pool, "init_done", 11)
        pool.memset(ctb[:, :, :, :], 0.0).then_inc(sm["init_done"], 1)
        pool.memset(zero1[:, :], 0.0).then_inc(sm["init_done"], 1)
        pool.memset(ecR[:, :, :], 0.0).then_inc(sm["init_done"], 1)
        wait(pool, "init_done", 14)
        pool.memset(ctb[:, :, :, ONE_ROW:ONE_ROW + 1], 1.0).then_inc(sm["init_done"], 1)
        wait(pool, "init_done", 15)

    def pe_prep(pe, n):
        if n == 0:
            wait(pe, "weights_in", 16 * N_LOADS)
            wait(pe, "init_done", 15)
            wait(pe, "prep_copied", 1)
            for c in range(2):
                mm = pe.transpose(G[0:KC, 4 * c:4 * c + 4], ec[:, c * KC:(c + 1) * KC], ident[0:4, 0:4])
            mm.then_inc(sm["pe_prep"], 1)
        if n == 1:
            wait(pe, "prep_copied", 3)
            wait(pe, "mats_ready", 2)
            for c in range(2):
                pe.matmul(G[0:SC, 0:16], ones[0:KC, 0:SC], ecP[:, c], start=(c == 0), stop=(c == 1))
            for c in range(2):
                pe.matmul(F[0:ROWS, 0:512], ecR[:, c], wqk[:, c], start=(c == 0), stop=False)
            pe.matmul(F[0:ROWS, 0:512], place1[:, :], onerow[:, :], start=False, stop=True)
            for h in range(HEADS):
                for c in range(2):
                    mm = pe.matmul(G[0:HD, 32 + 4 * h:36 + 4 * h], wv[:, c, h * HD:(h + 1) * HD], ecT[:, c],
                                   start=(c == 0), stop=(c == 1))
            mm.then_inc(sm["pe_prep"], 1)
        if n == 2:
            wait(pe, "prep_copied", 4)
            for h in range(HEADS):
                pe.matmul(G[0:16, 0:DIM], avT[:, h], wo[:, h], start=(h == 0), stop=(h == HEADS - 1))
            for c in range(2):
                pe.matmul(F[0:ROWS, 0:DIM], ecR[:, c], wg[:, c], start=(c == 0), stop=(c == 1))
            mm = pe.matmul(F[0:ROWS, DIM:2 * DIM], place[:, :], e4[:, :], start=True, stop=True)
            mm.then_inc(sm["pe_prep"], 1)

    def dve_prep(dve, n):
        if n == 0:
            wait(dve, "weights_in", 16 * N_LOADS)
            wait(dve, "init_done", 15)
            st = Steps(dve, sm["prep_steps"])
            st(dve.tensor_reduce(e4s[:, 0:1], e4[:, :], AX.X, ALU.add))
            st(dve.tensor_scalar(e4s[:, 1:2], e4s[:, 0:1], -1.0 / DIM, None, ALU.mult))
            dve.tensor_scalar(ec[:, :], e4[:, :], e4s[:, 1:2], None, ALU.add).then_inc(sm["prep_copied"], 1)
        if n == 1:
            wait(dve, "pe_prep", 1)
            dve.tensor_copy(ecT[:, :, :], G[0:KC, 0:8].rearrange("p (c j) -> p c j", c=2)).then_inc(sm["prep_copied"], 1)
            wait(dve, "prep_copied", 2)
            for c in range(2):
                rows = ecT[:, c].unsqueeze(2).to_broadcast([KC, 4, 4])
                cols = ecT[:, c].unsqueeze(1).to_broadcast([KC, 4, 4])
                ins = dve.scalar_tensor_tensor(out=ecP[:, c].rearrange("p (i j) -> p i j", i=4), in0=rows, scalar=1.0 / DIM,
                                               in1=cols, op0=ALU.mult, op1=ALU.mult)
                dve.tensor_copy(ecR[:, c, 0:24].rearrange("p (g j) -> p g j", g=6), ecT[:, c].unsqueeze(1).to_broadcast([KC, 6, 4]))\
                    .then_inc(sm["mats_ready"], 1)
            wait(dve, "mats_ready", 2)
            ins.then_inc(sm["prep_copied"], 1)
        if n == 2:
            wait(dve, "pe_prep", 2)
            dve.tensor_copy(gram[:, :], G[0:SC, 0:16]).then_inc(sm["mats_ready"], 1)
            dve.tensor_copy(mall[:, 0:512], F[0:ROWS, 0:512]).then_inc(sm["mats_ready"], 1)
            dve.tensor_copy(identb[:, :], ident[:, :]).then_inc(sm["mats_ready"], 1)
            wait(dve, "mats_ready", 5)
            for h in range(HEADS):
                ins = dve.tensor_copy(avT[:, h, 4 * h:4 * h + 4], G[0:HD, 32 + 4 * h:36 + 4 * h])
            ins.then_inc(sm["prep_copied"], 1)
        if n == 3:
            wait(dve, "pe_prep", 3)
            dve.tensor_copy(mo[64:80, :], G[0:16, 0:DIM]).then_inc(sm["mats_ready"], 1)
            st = Steps(dve, sm["prep_steps"], 2)
            st(dve.tensor_copy(mall[:, 512:MALL], F[0:ROWS, 0:2 * DIM]))
            st(dve.tensor_copy(m1[:, :], mall[:, :]))
            st(dve.tensor_tensor(mall[:, :], mall[:, :], m1[:, :], ALU.subtract))
            st(dve.tensor_copy(m2[:, :], mall[:, :]))
            st(dve.tensor_tensor(mall[:, :], mall[:, :], m2[:, :], ALU.subtract))
            st(dve.tensor_scalar(mb[:, :], mall[:, :], parts[:, 2:3], None, ALU.mult))
            st(dve.scalar_tensor_tensor(out=mb[:, :], in0=m2[:, :], scalar=parts[:, 1:2], in1=mb[:, :],
                                        op0=ALU.mult, op1=ALU.add))
            dve.scalar_tensor_tensor(out=mb[:, :], in0=m1[:, :], scalar=parts[:, 0:1], in1=mb[:, :],
                                     op0=ALU.mult, op1=ALU.add).then_inc(sm["mats_ready"], 1)

    Z_STEPS = 17

    def pool_z(pool, b, par):
        step = Steps(pool, sm["z_steps"], b * Z_STEPS)
        sv = sums[:, par].rearrange("p (c k) -> p c k", c=2)
        z, u = zu[:, par, 1:4:2], zu[:, par, 0:4:2]
        pool.wait_ge(seg["enm_ready"], b + 1)
        wait(pool, "tot_copied", 2 * b + 2)
        step(pool.tensor_tensor(den0[:, :], ntok[:, :], sv[:, :, 4], ALU.subtract))
        step(pool.tensor_tensor(den0[:, :], den0[:, :], enm[:, par:par + 1].to_broadcast([SC, 2]), ALU.mult))
        step(pool.tensor_tensor(den0[:, :], den0[:, :], sv[:, :, 0], ALU.add))
        step(pool.tensor_tensor(den0[:, :], den0[:, :], minus1[0:SC, :], ALU.pow))
        step(pool.tensor_tensor(z[:, :, 0:3], sv[:, :, 1:4], den0[:, :].unsqueeze(2).to_broadcast([SC, 2, 3]), ALU.mult))
        for c in range(2):
            ins = pool.tensor_tensor(quad[:, c].rearrange("p (i j) -> p i j", i=4), z[:, c].unsqueeze(2).to_broadcast([SC, 4, 4]),
                                     z[:, c].unsqueeze(1).to_broadcast([SC, 4, 4]), ALU.mult)
        step(ins)
        step(pool.tensor_tensor(quad[:, :, :], quad[:, :, :], gram[:, :].unsqueeze(1).to_broadcast([SC, 2, 16]), ALU.mult))
        for m in (8, 4, 2):
            step(pool.tensor_tensor(quad[:, :, 0:m], quad[:, :, 0:m], quad[:, :, m:2 * m], ALU.add))
        step(pool.tensor_tensor(zvar[:, :], quad[:, :, 0], quad[:, :, 1], ALU.add))
        step(pool.tensor_tensor(zvar[:, :], zvar[:, :], eps[:, :], ALU.add))
        step(pool.tensor_tensor(zrstd[:, :], zvar[:, :], mhalf[:, :], ALU.pow))
        step(pool.tensor_tensor(u, z, zrstd[:, :].unsqueeze(2).to_broadcast([SC, 2, 4]), ALU.mult))
        wait(pool, "t2_done", b - 1)
        v = zu[:, par]
        p = ctb[:, par].rearrange("p c (h n) -> p (c h) n", h=2)[:, :, 0:24].rearrange("p a (g j) -> p a g j", g=6)

        rounded = zero1[:, 0:1].unsqueeze(2).to_broadcast([SC, 4, 4])
        for g in range(3):
            ins = pool.tensor_tensor(p[:, :, g], v, rounded, ALU.add)
        step(ins)
        step(pool.tensor_tensor(zres[:, :, :], v, p[:, :, 0], ALU.subtract))
        for g in (3, 4):
            ins = pool.tensor_tensor(p[:, :, g], zres[:, :, :], rounded, ALU.add)
        step(ins)
        pool.tensor_tensor(ct[:, par, :, 0:4], u, rounded[:, 0:2], ALU.add)
        pool.tensor_tensor(p[:, :, 5], zres[:, :, :], p[:, :, 3], ALU.subtract).then_inc(sm["placed"], 1)

    def pe_t1(pe, b, par):
        wait(pe, "placed", b + 1)
        wait(pe, "xt_ready", b - 1)
        for c in range(2):
            mm = pe.matmul(G[0:ROWS, SC * c:SC * (c + 1)], ctb[:, par, c], identb[0:SC, 0:SC], start=True, stop=True)
        mm.then_inc(sm["t1_done"], 1)

    def act_ct1(act, b, par):
        wait(act, "t1_done", b + 1)
        act.copy(cTb[:, par], G[0:ROWS, 0:S]).then_inc(sm["ct1_ready"], 1)

    def pe_qk(pe, b, par, hp):
        wait(pe, "ct1_ready", b + 1)
        if hp == 1:
            wait(pe, "elu_ready", 2 * b + 1)
        for j in range(2):
            mm = pe.matmul(G[:, j * S:(j + 1) * S], mb[:, 256 * j + 128 * hp:256 * j + 128 * (hp + 1)], cTb[:, par],
                           start=True, stop=True)
        mm.then_inc(sm["qk_done"], 1)

    def act_elu(act, b, hp):
        wait(act, "qk_done", 2 * b + hp + 1)
        act.activation(expx[:, hp], G[:, 0:2 * S], ACT.Exp, bias=minus1[:, 0:1]).then_inc(sm["er_ready"], 1)

    def dve_elu(dve, b, hp):
        wait(dve, "er_ready", 2 * b + hp + 1)
        dve.scalar_tensor_tensor(out=qk[:, hp], in0=G[:, 0:2 * S], scalar=1.0, in1=expx[:, hp],
                                 op0=ALU.max, op1=ALU.min).then_inc(sm["elu_ready"], 1)

    def pe_scores(pe, b, h):
        hp, r = h // 2, h % 2
        wait(pe, "elu_ready", 2 * b + 2)
        if h == 0:
            wait(pe, "h1_ready", b)
        else:
            wait(pe, "at_copied", HEADS * b + h)
        rows = slice(HD * r, HD * (r + 1))
        q, k = qk[rows, hp, 0:S], qk[rows, hp, S:2 * S]
        pe.matmul(G[0:SC, 0:S], k[:, 0:SC], q, start=True, stop=True)
        pe.matmul(G[0:SC, S:S + SC], k[:, SC:S], q[:, SC:S], start=True, stop=True).then_inc(sm["at_done"], 1)

    def act_scores(act, b, h):
        wait(act, "at_done", HEADS * b + h + 1)
        act.copy(aT[:, h], G[0:SC, 0:3 * SC]).then_inc(sm["at_copied"], 1)

    def pool_mask(pool, b, h):
        wait(pool, "at_copied", HEADS * b + h + 1)
        v = aT[:, h].rearrange("p (g i) -> p g i", g=3)[:, 0:3:2]
        pool.tensor_tensor(v, v, tri[0:SC].unsqueeze(1).to_broadcast([SC, 2, SC]), ALU.mult).then_inc(sm["masked"], 1)

    def pe_sums2(pe, b, par, h):
        wait(pe, "masked", HEADS * (b + 1))
        o = [G[0:SC, 20 * c + 5 * h:20 * c + 5 * h + 5] for c in range(2)]
        pe.matmul(o[0], aT[:, h, 0:SC], ct[:, par, 0, 0:5], start=True, stop=True)
        pe.matmul(o[1], aT[:, h, SC:2 * SC], ct[:, par, 0, 0:5], start=True, stop=False)
        mm = pe.matmul(o[1], aT[:, h, 2 * SC:3 * SC], ct[:, par, 1, 0:5], start=False, stop=True)
        if h == HEADS - 1:
            mm.then_inc(sm["n_done"], 1)

    def dve_y(dve, b, par):
        wait(dve, "n_done", b + 1)
        st = Steps(dve, sm["y_steps"], 2 * b)
        num = G[0:SC, 0:40].rearrange("p (c h k) -> p c h k", c=2, h=HEADS)
        st(dve.tensor_scalar(den[:, :, :], num[:, :, :, 4], DEN_MIN, None, ALU.max))
        st(dve.reciprocal(rden[:, :, :], den[:, :, :]))
        out = ct[:, par, :, 64:80].rearrange("p c (h k) -> p c h k", h=HEADS)
        dve.tensor_tensor(out, num[:, :, :, 0:4], rden[:, :, :].unsqueeze(3).to_broadcast([SC, 2, HEADS, 4]),
                          ALU.mult).then_inc(sm["y_ready"], 1)

    def pe_t2(pe, b, par):
        wait(pe, "y_ready", b + 1)
        for c in range(2):
            mm = pe.transpose(G[0:CROWS, SC * c:SC * (c + 1)], ct[:, par, c], ident[0:SC, 0:SC])
        mm.then_inc(sm["t2_done"], 1)

    def act_ct2(act, b):
        wait(act, "t2_done", b + 1)
        act.copy(cT2[:, :], G[0:CROWS, 0:S]).then_inc(sm["ct2_ready"], 1)

    def pe_h(pe, b, par):
        wait(pe, "gated_ready", 2 * b + 2)
        for c in range(2):
            mm = pe.matmul(G[0:SC, DIM * c:DIM * (c + 1)], cTb[:, par, SC * c:SC * (c + 1)], mb[:, 512 + DIM:MALL],
                           start=True, stop=True)
        mm.then_inc(sm["h_done"], 1)

    def pe_out(pe, b, par, c):
        wait(pe, "ct2_ready", b + 1)
        if c == 0:
            wait(pe, "elu_ready", min(2 * b + 4, 2 * B) if isinstance(b, int) else 2 * b + 4)
        else:
            wait(pe, "gated_ready", 2 * b + 1)
        pe.matmul(G[0:SC, DIM:2 * DIM], cTb[:, par, SC * c:SC * (c + 1)], mb[:, 512:512 + DIM], start=True, stop=True)
        pe.matmul(G[0:SC, 0:DIM], cT2[:, SC * c:SC * (c + 1)], mo[:, :], start=True, stop=True).then_inc(sm["o_done"], 1)

    def act_gate(act, b, c):
        wait(act, "o_done", 2 * b + c + 1)
        act.activation(th[:, c], G[0:SC, DIM:2 * DIM], ACT.Tanh, scale=0.5).then_inc(sm["th_ready"], 1)

    def dve_gated(dve, b, c):
        wait(dve, "th_ready", 2 * b + c + 1)
        dve.scalar_tensor_tensor(out=gated[:, c], in0=th[:, c], scalar=1.0, in1=G[0:SC, 0:DIM],
                                 op0=ALU.add, op1=ALU.mult).then_inc(sm["gated_ready"], 1)

    def dve_h1(dve, b, par):
        wait(dve, "gated_ready", 2 * b + 2)
        wait(dve, "h_done", b + 1)
        dve.scalar_tensor_tensor(out=h1[:, par], in0=gated[:, :, :], scalar=0.5,
                                 in1=G[0:SC, 0:2 * DIM].rearrange("p (c d) -> p c d", c=2),
                                 op0=ALU.mult, op1=ALU.add).then_inc(sm["h1_ready"], 1)
        wait(dve, "h1_ready", b + 1)
        for c in range(2):
            dve.bn_stats(bns[:, c], h1[:, par, c]).then_inc(sm["var_steps"], 1)
        wait(dve, "var_steps", 2 * b + 2)

    def dve_aggregate(dve, b):
        for c in range(2):
            ins = dve.bn_aggr(mv[:, c], bns[:, c])
        ins.then_inc(sm["var_ready"], 1)

    def pool_norm(pool, b, par):
        wait(pool, "var_ready", b + 1)
        pool.tensor_tensor(vare[:, :], mv[:, :, 1], eps[:, :], ALU.add).then_inc(sm["rstd_steps"], 1)
        wait(pool, "rstd_steps", b + 1)
        pool.tensor_tensor(rstd[:, :], vare[:, :], mhalf[:, :], ALU.pow).then_inc(sm["rstd_ready"], 1)
        wait(pool, "t3_done", b)
        pool.tensor_tensor(x2[:, :, :], h1[:, par], mv[:, :, 0:1].to_broadcast([SC, 2, DIM]), ALU.subtract)\
            .then_inc(sm["x2_steps"], 1)
        wait(pool, "x2_steps", b + 1)
        wait(pool, "rstd_ready", b + 1)
        pool.tensor_tensor(x2[:, :, :], x2[:, :, :], rstd[:, :].unsqueeze(2).to_broadcast([SC, 2, DIM]), ALU.mult)\
            .then_inc(sm["x2_ready"], 1)

    def pe_t3(pe, b):
        wait(pe, "x2_ready", b + 1)
        wait(pe, "ct2_ready", min(b + 2, B) if isinstance(b, int) else b + 2)
        for kc in range(2):
            for c in range(2):
                mm = pe.transpose(G[0:KC, S * kc + SC * c:S * kc + SC * (c + 1)], x2[:, c, KC * kc:KC * (kc + 1)],
                                  ident[0:SC, 0:SC])
        mm.then_inc(sm["t3_done"], 1)

    def act_xt(act, b, par):
        wait(act, "t3_done", b + 1)
        wait(act, "ff_done", 8 * (b - 1))
        act.copy(xT[0:KC, par].rearrange("p k s -> p (k s)"), G[0:KC, 0:2 * S]).then_inc(sm["xt_ready"], 1)

    def rows_of(t, par, kc, c):
        return t[:, par, kc, SC * c:SC * (c + 1)]

    def pe_router(pe, b, par, kept):
        wait(pe, "xt_ready", b + 1)
        wait(pe, "mixed", 16 * b)
        wait(pe, "tot_copied", 2 * kept)
        for c in range(2):
            for kc in range(2):
                mm = pe.matmul(F[0:SC, EXPERTS * c:EXPERTS * (c + 1)], rows_of(xT, par, kc, c), wrt[:, kc],
                               start=(kc == 0), stop=(kc == 1))
        mm.then_inc(sm["r_done"], 1)

    def dve_router1(dve, b):
        wait(dve, "r_done", b + 1)
        dve.tensor_copy(rs[:, :, 0:EXPERTS], F[0:SC, 0:2 * EXPERTS].rearrange("p (c e) -> p c e", c=2)).then_inc(sm["r_steps"], 1)
        for c in range(2):
            ins = dve.max(rs[:, c, 8:16], F[0:SC, EXPERTS * c:EXPERTS * (c + 1)])
        ins.then_inc(sm["r_steps"], 1)
        wait(dve, "r_steps", b * N_RSTEPS + 2)
        dve.tensor_tensor(rd[:, :, :], rs[:, :, 0:10], rs[:, :, 8:9].to_broadcast([SC, 2, 10]), ALU.subtract)\
           .then_inc(sm["rd_ready"], 1)

    def act_router(act, b):
        wait(act, "rd_ready", b + 1)
        act.activation(re[:, :, :], rd[:, :, :], ACT.Exp).then_inc(sm["re_ready"], 1)

    N_RSTEPS = 5

    def dve_router2(dve, b, par):
        wait(dve, "re_ready", b + 1)
        st = Steps(dve, sm["r_steps"], b * N_RSTEPS + 2)
        dve.tensor_reduce(rsum[:, :], re[:, :, 0:EXPERTS], AX.X, ALU.add)
        dve.tensor_tensor(rmask[:, :, :], rd[:, :, 0:EXPERTS], rd[:, :, 9:10].to_broadcast([SC, 2, EXPERTS]), ALU.is_ge)
        st(dve.tensor_tensor(rtop[:, :], re[:, :, 8], re[:, :, 9], ALU.add))
        dve.tensor_tensor(rw[:, :, :], rmask[:, :, :], re[:, :, 0:EXPERTS], ALU.mult)
        st(dve.scalar_tensor_tensor(out=rnorm[:, :], in0=rsum[:, :], scalar=TOP_EPS, in1=rtop[:, :], op0=ALU.mult, op1=ALU.add))
        st(dve.reciprocal(rinv[:, :], rnorm[:, :]))
        dve.tensor_tensor(wt[:, par], rw[:, :, :], rinv[:, :].unsqueeze(2).to_broadcast([SC, 2, EXPERTS]), ALU.mult)\
           .then_inc(sm["w_ready"], 1)

    def pe_experts(pe, b, par, n, q):
        c, pair = n // 4, n % 4
        r, kc = q // 2, q % 2
        if q == 0:
            wait(pe, "mixed", 16 * b + 2 * n)
            if n == 0:
                wait(pe, "rd_ready", b + 1)
        e = 2 * pair + r
        mm = pe.matmul(F[0:SC, DIM * r:DIM * (r + 1)], rows_of(xT, par, kc, c), wff[:, kc, DIM * e:DIM * (e + 1)],
                       start=(kc == 0), stop=(kc == 1))
        if q == 3:
            mm.then_inc(sm["ff_done"], 1)

    def dve_mix(dve, b, par, n, r):
        c, pair = n // 4, n % 4
        wait(dve, "ff_done", 8 * b + n + 1)
        if n == 0 and r == 0:
            wait(dve, "w_ready", b + 1)
            wait(dve, "out_ready", 2 * b - 2)
        e, mix = 2 * pair + r, (mixa, mixb)[r]
        y, w = F[0:SC, DIM * r:DIM * (r + 1)], wt[:, par, c, e:e + 1]
        if pair:
            wait(dve, "mixed", 16 * b + 2 * n - 1 + r)
        if pair == 0 and r == 1:
            ins = dve.tensor_scalar(mix[:, par, c], y, w, None, ALU.mult)
        else:
            ins = dve.scalar_tensor_tensor(out=mix[:, par, c], in0=y, scalar=w, in1=(mix if pair else h1)[:, par, c],
                                           op0=ALU.mult, op1=ALU.add)
        ins.then_inc(sm["mixed"], 1)

    def pool_out(pool, b, par, c):
        wait(pool, "mixed", 16 * b + 8 * (c + 1))
        wait(pool, f"stored{par}", 8 * (b - par))
        pool.tensor_tensor(outb[:, par, c], mixa[:, par, c], mixb[:, par, c], ALU.add).then_inc(sm["out_ready"], 1)

    def sp_store(sp, b, par):
        wait(sp, "out_ready", 2 * b + 2)
        sp.dma_start(out_d[b].rearrange("(c p) d -> p c d", c=2), outb[:, par]).then_inc(sm[f"stored{par}"], 16)

    def sp_stored(sp):
        for par in range(2):
            wait(sp, f"stored{par}", 8 * B)

    return dict(sp_weights=sp_weights, sp_store=sp_store, sp_stored=sp_stored, pool_init=pool_init, pool_z=pool_z,
                pool_mask=pool_mask, pool_norm=pool_norm, pool_out=pool_out,
                pe_prep=pe_prep, pe_t1=pe_t1, pe_qk=pe_qk, pe_scores=pe_scores, pe_sums2=pe_sums2, pe_t2=pe_t2,
                pe_h=pe_h, pe_out=pe_out, pe_t3=pe_t3, pe_router=pe_router, pe_experts=pe_experts,
                act_ct1=act_ct1, act_elu=act_elu, act_scores=act_scores, act_ct2=act_ct2, act_gate=act_gate,
                act_xt=act_xt, act_router=act_router,
                dve_prep=dve_prep, dve_elu=dve_elu, dve_y=dve_y, dve_gated=dve_gated, dve_h1=dve_h1,
                dve_aggregate=dve_aggregate, dve_router1=dve_router1, dve_router2=dve_router2,
                dve_mix=dve_mix, mats_ready=sm["mats_ready"], mixed=sm["mixed"])


def build(nc, a, out_d, n_images):
    B = n_images
    with ExitStack() as ctx:
        psum = ctx.enter_context(nc.psum_tensor("psum", [P, 8, 512], F32))[:, :, :]
        pad_d = nc.dram_tensor("planes_pad", [2, PLANES, (H + 2) * PW + 60], BF16).ap()
        g = segment_sums(nc, ctx, a["x"], a["conv_w108"], a["conv_b"], a["score_w"], a["keep"], a["sel"],
                                           pad_d, psum, psum[:, SLOTS + 2])
        t = layer(nc, ctx, B, a, out_d, a["ident"], a["tri"], psum, g)
        block = ctx.enter_context(nc.Block())

        def rounds(eng, one_round):
            def at(r):
                one_round(eng, r // 2, r % 2, r, [0 <= r - j < B for j in range(5)], r + 1 < B, r + 2 < B)

            head = min(6, B)
            for r in range(head):
                at(r)
            if B - 2 > head:
                with eng.Fori(head // 2, B // 2 - 1) as i:
                    for par in range(2):
                        one_round(eng, i, par, None, [True] * 5, True, True)
            for r in range(max(head, B - 2), B + 4):
                at(r)

        def sp_round(sp, i, par, r, does, more, more2):
            if r == 0:
                sp.wait_ge(g["ones_odd"], 1)
            if more:
                g["sp_patches"](sp, *image(i, par, 1))
            if more2:
                g["sp_load_x"](sp, i + 1, par)
            if does[4]:
                t["sp_store"](sp, 2 * i + par - 4, par)

        def pool_round(pool, i, par, r, does, more, more2):
            b = 2 * i + par
            if more:
                g["pool_split"](pool, *image(i, par, 1))
            if r == 1:
                pool.wait_ge(t["mats_ready"], 7)
            if does[1]:
                t["pool_z"](pool, b - 1, 1 - par)
            if more:
                g["pool_features"](pool, *image(i, par, 1))
            if does[4]:
                t["pool_out"](pool, b - 4, par, 0)
            if does[3]:
                t["pool_norm"](pool, b - 3, 1 - par)
            if does[2]:
                for h in range(HEADS):
                    t["pool_mask"](pool, b - 2, h)
            if does[4]:
                t["pool_out"](pool, b - 4, par, 1)

        def pe_round(pe, i, par, r, does, more, more2):
            b = 2 * i + par
            kept = b if r is None else min(r, B)
            if r == 2:
                pe.wait_ge(t["mats_ready"], 7)
            for k in range(NG):
                if does[0]:
                    g["pe_group"](pe, i, par, k, more)
                if r == 0 and k in PE_AT["prep"]:
                    t["pe_prep"](pe, PE_AT["prep"].index(k))
                if does[3] and k == PE_AT["t2"]:
                    t["pe_t2"](pe, b - 3, 1 - par)
                if does[4] and k == PE_AT["t3"]:
                    t["pe_t3"](pe, b - 4)
                if does[1] and k == PE_AT["total"]:
                    need(pe, t["mixed"], 16 * (b - 4))
                    g["pe_total"](pe, b - 1, 1 - par)
                if does[4] and k == PE_AT["router"]:
                    t["pe_router"](pe, b - 4, par, kept)
                if does[3]:
                    if k in PE_AT["out"]:
                        t["pe_out"](pe, b - 3, 1 - par, PE_AT["out"].index(k))
                    if k == PE_AT["h"]:
                        t["pe_h"](pe, b - 3, 1 - par)
                if does[2]:
                    if k == PE_AT["t1"]:
                        t["pe_t1"](pe, b - 2, par)
                    if k in PE_AT["qk"]:
                        t["pe_qk"](pe, b - 2, par, PE_AT["qk"].index(k))
                    if k in PE_AT["scores"]:
                        t["pe_scores"](pe, b - 2, PE_AT["scores"].index(k))
                    if k in PE_AT["sums"]:
                        t["pe_sums2"](pe, b - 2, par, PE_AT["sums"].index(k))
                if does[4] and k in PE_AT["experts"]:
                    at = PE_AT["experts"].index(k)
                    t["pe_experts"](pe, b - 4, par, at // 4, at % 4)

        def act_round(act, i, par, r, does, more, more2):
            b = 2 * i + par
            for k in range(NG):
                if does[0]:
                    g["act_group"](act, b, k)
                if more and k == ACT_AT["e"]:
                    g["act_e"](act, b + 1, 1 - par)
                if does[2]:
                    if k == ACT_AT["ct1"]:
                        t["act_ct1"](act, b - 2, par)
                    if k in ACT_AT["elu"]:
                        t["act_elu"](act, b - 2, ACT_AT["elu"].index(k))
                    if k in ACT_AT["scores"]:
                        t["act_scores"](act, b - 2, ACT_AT["scores"].index(k))
                if does[3]:
                    if k == ACT_AT["ct2"]:
                        t["act_ct2"](act, b - 3)
                    if k in ACT_AT["gate"]:
                        t["act_gate"](act, b - 3, ACT_AT["gate"].index(k))
                if does[4]:
                    if k == ACT_AT["xt"]:
                        t["act_xt"](act, b - 4, par)
                    if k == ACT_AT["router"]:
                        t["act_router"](act, b - 4)

        def dve_round(dve, i, par, r, does, more, more2):
            b = 2 * i + par
            for k in range(NG):
                if does[0]:
                    g["dve_group"](dve, b, k)
                if r == 0 and k in DVE_AT["prep"]:
                    t["dve_prep"](dve, DVE_AT["prep"].index(k))
                if does[1] and k == DVE_AT["copy"]:
                    g["dve_copy_acc"](dve, b - 1, 1 - par)
                if does[1] and k == DVE_AT["keep"]:
                    g["dve_keep"](dve, b - 1, 1 - par)
                if more and k == DVE_AT["pmax"]:
                    g["dve_pmax"](dve, b + 1, 1 - par)
                if more and k == DVE_AT["negm"]:
                    g["dve_negm"](dve, b + 1, 1 - par)
                if does[4] and k == DVE_AT["router1"]:
                    t["dve_router1"](dve, b - 4)
                if does[4] and k == DVE_AT["router2"]:
                    t["dve_router2"](dve, b - 4, par)
                if does[2]:
                    if k in DVE_AT["elu"]:
                        t["dve_elu"](dve, b - 2, DVE_AT["elu"].index(k))
                    if k == DVE_AT["y"]:
                        t["dve_y"](dve, b - 2, par)
                if does[3]:
                    if k in DVE_AT["gated"]:
                        t["dve_gated"](dve, b - 3, DVE_AT["gated"].index(k))
                    if k == DVE_AT["h1"]:
                        t["dve_h1"](dve, b - 3, 1 - par)
                    if k == DVE_AT["aggregate"]:
                        t["dve_aggregate"](dve, b - 3)
                if does[4] and k in DVE_AT["mix"]:
                    at = DVE_AT["mix"].index(k)
                    t["dve_mix"](dve, b - 4, par, at // 2, at % 2)

        @block.sync
        def _(sp):
            g["sp_constants"](sp)
            g["sp_start"](sp)
            t["sp_weights"](sp)
            rounds(sp, sp_round)
            t["sp_stored"](sp)

        @block.gpsimd
        def _(pool):
            g["pool_init"](pool)
            g["pool_split"](pool, 0, 0)
            g["pool_ones"](pool)
            t["pool_init"](pool)
            g["pool_features"](pool, 0, 0)
            rounds(pool, pool_round)

        @block.tensor
        def _(pe):
            g["pe_start"](pe)
            rounds(pe, pe_round)

        @block.scalar
        def _(act):
            act.preload_act_table(ACT.Exp)
            g["act_e"](act, 0, 0)
            rounds(act, act_round)

        @block.vector
        def _(dve):
            g["dve_start"](dve)
            rounds(dve, dve_round)


def kernel(**inputs):
    import numpy as _np
    import concourse.bacc as _bacc
    from concourse import mybir as _mybir
    from concourse.bass_utils import run_bass_kernel_spmd as _run

    given = {k: _np.asarray(v) for k, v in inputs.items()}
    arrays = layout(given)
    n_images = given["x"].shape[0]
    nc = _bacc.Bacc("TRN2", target_bir_lowering=False, num_devices=1)
    aps = {n: nc.dram_tensor(f"in_{n}", v.shape, _mybir.dt.from_np(v.dtype), kind="ExternalInput").ap()
           for n, v in arrays.items()}
    out_d = nc.dram_tensor("out", (n_images, S, DIM), _mybir.dt.float32, kind="ExternalOutput").ap()
    build(nc, aps, out_d, n_images)
    r = _run(nc, [{f"in_{n}": v for n, v in arrays.items()}], core_ids=[0])
    return r.results[0]["out"]


def layout(given):
    keep, sel, ident, tri, place, parts = constants()
    w = given["L0_tok_conv_w"].transpose(2, 3, 1, 0).reshape(TAPS, 1, C, S)
    arrays = {
        "x": given["x"],
        "conv_w108": np.broadcast_to(w, (TAPS, PLANES // C, C, S)).reshape(TAPS * PLANES, S),
        "conv_b": given["L0_tok_conv_b"],
        "score_w": given["L0_tok_score_w"],
        "embed_w": given["L0_tok_embed_w"],
        "embed_b": given["L0_tok_embed_b"],
        "Wq": given["L0_attn_Wq"], "Wk": given["L0_attn_Wk"], "Wv": given["L0_attn_Wv"],
        "Wo": given["L0_attn_Wo"], "Wg": given["L0_attn_Wg"],
        "router_wT": given["L0_ffn_router_w"].T,
        "router_b": given["L0_ffn_router_b"],
        "expert_wT": given["L0_ffn_expert_w"].transpose(0, 2, 1),
        "expert_b": given["L0_ffn_expert_b"],
        "keep": keep, "sel": sel, "ident": ident, "tri": tri, "place": place, "parts": parts,
    }
    return {n: np.ascontiguousarray(v) for n, v in arrays.items()}
```
